# Optimizing a Trainium2 kernel written in Bass

```python
import numpy as np
import jax
import jax.numpy as jnp

def _softmax(x, axis=-1):
    return jax.nn.softmax(x, axis=axis)

def _gelu(x):
    return jax.nn.gelu(x, approximate=True)

def _silu(x):
    return jax.nn.silu(x)

def _sigmoid(x):
    return jax.nn.sigmoid(x)

def _layernorm(x, axis=-1, eps=1e-05):
    m = jnp.mean(x, axis=axis, keepdims=True)
    v = jnp.var(x, axis=axis, keepdims=True)
    return (x - m) / jnp.sqrt(v + eps)

def _scatter_add(tgt, idx, src, axis=0):
    return tgt.at[idx].add(src)

def _segment_sum(src, seg, n):
    return jax.ops.segment_sum(src, seg, n)
kernel_name = 'mk_macaron_d1_jaxref_r8_618fbc'

def setup_inputs(seed: int=0):
    np.random.seed(seed)
    _w = jnp.asarray

    def _L0_attn_setup():
        import jax, jax.numpy as jnp
        import numpy as np
        B, L, D_MODEL = (4, 256, 128)
        N_HEADS, FEAT, HEAD_DIM = (16, 16, 64)
        CHUNK = 128
        EPS = 1e-12

        def taylor_exp(x):
            f = x.shape[-1]
            r2 = jnp.sqrt(jnp.asarray(2.0, x.dtype))
            rd = jnp.sqrt(jnp.asarray(float(f), x.dtype))
            rrd = jnp.sqrt(rd)
            x2 = (x[..., :, None] * x[..., None, :]).reshape(*x.shape[:-1], f * f) / r2
            ones = jnp.ones_like(x[..., :1])
            return jnp.concatenate([ones, x / rrd, x2 / rd], axis=-1)
        key = jax.random.key(seed)
        k1, k2, k3, k4, k5 = jax.random.split(key, 5)
        s = 0.02
        return {'hidden_states': jax.random.normal(k1, (B, L, D_MODEL), jnp.float32), 'Wq': jax.random.normal(k2, (N_HEADS * FEAT, D_MODEL), jnp.float32) * s, 'Wk': jax.random.normal(k3, (N_HEADS * FEAT, D_MODEL), jnp.float32) * s, 'Wv': jax.random.normal(k4, (N_HEADS * HEAD_DIM, D_MODEL), jnp.float32) * s, 'Wo': jax.random.normal(k5, (D_MODEL, N_HEADS * HEAD_DIM), jnp.float32) * s}
    _L0_attn_in = _L0_attn_setup()

    def _L0_ffn_setup():
        import jax, jax.numpy as jnp
        import numpy as np
        B, S, D = (4, 256, 128)
        P = 9
        DM = D // 4
        EPS = 1e-05

        def _mix(x, mix_kernel):
            xp = jnp.pad(x, ((0, 0), (1, 1), (0, 0)))
            return mix_kernel[0] * xp[:, :-2] + mix_kernel[1] * xp[:, 1:-1] + mix_kernel[2] * xp[:, 2:]

        def _layernorm(h, gamma, beta):
            mu = jnp.mean(h, axis=-1, keepdims=True)
            var = jnp.var(h, axis=-1, keepdims=True)
            return (h - mu) * jax.lax.rsqrt(var + EPS) * gamma + beta
        key = jax.random.key(seed)
        ks = jax.random.split(key, 12)
        sc_in = 1.0 / np.sqrt(D)
        sc_mid = 1.0 / np.sqrt(DM)
        return {'x': jax.random.normal(ks[0], (B, S, D), dtype=jnp.float32), 'mix_kernel': jax.random.normal(ks[1], (3, D), dtype=jnp.float32) * 0.5, 'W1': jax.random.normal(ks[2], (P, D, DM), dtype=jnp.float32) * sc_in, 'b1': jnp.zeros((P, DM), dtype=jnp.float32), 'W2': jax.random.normal(ks[3], (P, DM, D), dtype=jnp.float32) * sc_mid, 'b2': jnp.zeros((P, D), dtype=jnp.float32), 'Wo1': jax.random.normal(ks[4], (D, DM), dtype=jnp.float32) * sc_in, 'bo1': jnp.zeros((DM,), dtype=jnp.float32), 'Wo2': jax.random.normal(ks[5], (DM, P), dtype=jnp.float32) * sc_mid, 'bo2': jnp.zeros((P,), dtype=jnp.float32), 'gamma': jnp.ones((D,), dtype=jnp.float32), 'beta': jnp.zeros((D,), dtype=jnp.float32)}
    _L0_ffn_in = _L0_ffn_setup()
    _d = {'L0_attn_hidden_states': _L0_attn_in['hidden_states'], 'L0_attn_Wq': _L0_attn_in['Wq'], 'L0_attn_Wk': _L0_attn_in['Wk'], 'L0_attn_Wv': _L0_attn_in['Wv'], 'L0_attn_Wo': _L0_attn_in['Wo'], 'L0_ffn_mix_kernel': _L0_ffn_in['mix_kernel'], 'L0_ffn_W1': _L0_ffn_in['W1'], 'L0_ffn_b1': _L0_ffn_in['b1'], 'L0_ffn_W2': _L0_ffn_in['W2'], 'L0_ffn_b2': _L0_ffn_in['b2'], 'L0_ffn_Wo1': _L0_ffn_in['Wo1'], 'L0_ffn_bo1': _L0_ffn_in['bo1'], 'L0_ffn_Wo2': _L0_ffn_in['Wo2'], 'L0_ffn_bo2': _L0_ffn_in['bo2'], 'L0_ffn_gamma': _L0_ffn_in['gamma'], 'L0_ffn_beta': _L0_ffn_in['beta']}
    _x0 = _d['L0_attn_hidden_states']
    _d['L0_attn_hidden_states'] = jax.random.normal(jax.random.fold_in(jax.random.key(seed), 1), (8, 256, 128), dtype=_x0.dtype)
    del _x0
    return _d

def reference(L0_attn_hidden_states, L0_attn_Wq, L0_attn_Wk, L0_attn_Wv, L0_attn_Wo, L0_ffn_mix_kernel, L0_ffn_W1, L0_ffn_b1, L0_ffn_W2, L0_ffn_b2, L0_ffn_Wo1, L0_ffn_bo1, L0_ffn_Wo2, L0_ffn_bo2, L0_ffn_gamma, L0_ffn_beta):

    def _L0_attn_ref(hidden_states, Wq, Wk, Wv, Wo):
        import jax, jax.numpy as jnp
        import numpy as np
        B, L, D_MODEL = (4, 256, 128)
        N_HEADS, FEAT, HEAD_DIM = (16, 16, 64)
        CHUNK = 128
        EPS = 1e-12

        def taylor_exp(x):
            f = x.shape[-1]
            r2 = jnp.sqrt(jnp.asarray(2.0, x.dtype))
            rd = jnp.sqrt(jnp.asarray(float(f), x.dtype))
            rrd = jnp.sqrt(rd)
            x2 = (x[..., :, None] * x[..., None, :]).reshape(*x.shape[:-1], f * f) / r2
            ones = jnp.ones_like(x[..., :1])
            return jnp.concatenate([ones, x / rrd, x2 / rd], axis=-1)
        b, l, _ = hidden_states.shape
        q = (hidden_states @ Wq.T).reshape(b, l, N_HEADS, FEAT).transpose(0, 2, 1, 3)
        k = (hidden_states @ Wk.T).reshape(b, l, N_HEADS, FEAT).transpose(0, 2, 1, 3)
        v = (hidden_states @ Wv.T).reshape(b, l, N_HEADS, HEAD_DIM).transpose(0, 2, 1, 3)
        qf = taylor_exp(q)
        kf = taylor_exp(k)
        De = qf.shape[-1]
        n = l // CHUNK
        qc = jnp.moveaxis(qf.reshape(b, N_HEADS, n, CHUNK, De), 2, 0)
        kc = jnp.moveaxis(kf.reshape(b, N_HEADS, n, CHUNK, De), 2, 0)
        vc = jnp.moveaxis(v.reshape(b, N_HEADS, n, CHUNK, HEAD_DIM), 2, 0)
        mask = jnp.tril(jnp.ones((CHUNK, CHUNK), qf.dtype))

        def step(carry, xs):
            S, z = carry
            qi, ki, vi = xs
            attn = jnp.einsum('bhid,bhjd->bhij', qi, ki) * mask
            num = jnp.einsum('bhij,bhje->bhie', attn, vi) + jnp.einsum('bhid,bhde->bhie', qi, S)
            den = attn.sum(-1) + jnp.einsum('bhid,bhd->bhi', qi, z)
            yi = num / (den[..., None] + EPS)
            S = S + jnp.einsum('bhjd,bhje->bhde', ki, vi)
            z = z + ki.sum(2)
            return ((S, z), yi)
        S0 = jnp.zeros((b, N_HEADS, De, HEAD_DIM), qf.dtype)
        z0 = jnp.zeros((b, N_HEADS, De), qf.dtype)
        _, ys = jax.lax.scan(step, (S0, z0), (qc, kc, vc))
        y = jnp.moveaxis(ys, 0, 2).reshape(b, N_HEADS, l, HEAD_DIM)
        y = y.transpose(0, 2, 1, 3).reshape(b, l, N_HEADS * HEAD_DIM)
        return y @ Wo.T

    def _L0_ffn_ref(x, mix_kernel, W1, b1, W2, b2, Wo1, bo1, Wo2, bo2, gamma, beta):
        import jax, jax.numpy as jnp
        import numpy as np
        B, S, D = (4, 256, 128)
        P = 9
        DM = D // 4
        EPS = 1e-05

        def _mix(x, mix_kernel):
            xp = jnp.pad(x, ((0, 0), (1, 1), (0, 0)))
            return mix_kernel[0] * xp[:, :-2] + mix_kernel[1] * xp[:, 1:-1] + mix_kernel[2] * xp[:, 2:]

        def _layernorm(h, gamma, beta):
            mu = jnp.mean(h, axis=-1, keepdims=True)
            var = jnp.var(h, axis=-1, keepdims=True)
            return (h - mu) * jax.lax.rsqrt(var + EPS) * gamma + beta
        x_mixed = _mix(x, mix_kernel)
        h = jnp.einsum('bsd,pdm->bspm', x_mixed, W1) + b1
        stacked_paths = jnp.einsum('bspm,pmd->bspd', h, W2) + b2
        scores = jnp.tanh(x_mixed @ Wo1 + bo1) @ Wo2 + bo2
        idx = jnp.argmax(scores, axis=-1)
        weights = jax.nn.one_hot(idx, P, dtype=stacked_paths.dtype)
        collapsed = jnp.einsum('bspd,bsp->bsd', stacked_paths, weights)
        return _layernorm(x + collapsed, gamma, beta)
    x = L0_attn_hidden_states
    x = x + 0.5 * _L0_ffn_ref(_layernorm(x, axis=-1), L0_ffn_mix_kernel, L0_ffn_W1, L0_ffn_b1, L0_ffn_W2, L0_ffn_b2, L0_ffn_Wo1, L0_ffn_bo1, L0_ffn_Wo2, L0_ffn_bo2, L0_ffn_gamma, L0_ffn_beta)
    x = x + _L0_attn_ref(_layernorm(x, axis=-1), L0_attn_Wq, L0_attn_Wk, L0_attn_Wv, L0_attn_Wo)
    x = x + 0.5 * _L0_ffn_ref(_layernorm(x, axis=-1), L0_ffn_mix_kernel, L0_ffn_W1, L0_ffn_b1, L0_ffn_W2, L0_ffn_b2, L0_ffn_Wo1, L0_ffn_bo1, L0_ffn_Wo2, L0_ffn_bo2, L0_ffn_gamma, L0_ffn_beta)
    return x

_drawn_inputs = setup_inputs


def setup_inputs(seed=0):
    import zlib

    import numpy as np

    out = dict(_drawn_inputs(seed))
    spreads = {'L0_ffn_b1': (0.0, 0.1),
     'L0_ffn_b2': (0.0, 0.1),
     'L0_ffn_bo1': (0.0, 0.1),
     'L0_ffn_bo2': (0.0, 0.1),
     'L0_ffn_gamma': (1.0, 0.2),
     'L0_ffn_beta': (0.0, 0.1)}
    factors = {'L0_attn_Wq': 6.984, 'L0_attn_Wk': 7.061}
    for name, (base, spread) in spreads.items():
        noise = np.random.default_rng([zlib.crc32(name.encode()), seed]).standard_normal(out[name].shape)
        drawn = base * np.exp(spread * noise) if base else spread * noise
        out[name] = jnp.asarray(drawn.astype(out[name].dtype))
    for name, factor in factors.items():
        out[name] = (out[name] * factor).astype(out[name].dtype)
    return out
```

```python
from contextlib import ExitStack

import concourse.bass as bass
from concourse import mybir

F32 = mybir.dt.float32
BF16 = mybir.dt.bfloat16
ALU = mybir.AluOpType
ACT = mybir.ActivationFunctionType
AX = mybir.AxisListType

P = 128
NSEQ, L, D = 8, 256, 128
NT = L // P
HEADS, FEAT, HD = 16, 16, 64
GROUP = 4
NG = HEADS // GROUP
HALF = HD // 2
PATHS, DM = 9, 32
HID = PATHS * DM
SLAB = 4
KCH = (PATHS + HID) // 3
QSLOT = (0, 0, 0, 1, 1, 2)
KSLOT = (0, 1, 2, 0, 1, 0)
NSLOT = len(QSLOT)
EPS_LN = 1e-5
EPS_DEN = 1e-12
LAST = NSEQ + 1

FFN_A = ["fxt", "th", "sc"]
BANK = {"fxt": 1, "th": 0, "sc": 1, "h0": 0, "h1": 1, "h2": 0, "h3": 1, "ht0": 0, "ht1": 1, "ht2": 0,
        "ht3": 1, "w2": 0, "b0": 1, "b1": 0, "o": 1, "ot": 0, "axt": 1, "q": 0, "k": 1, "v0": 0,
        "v1": 1, "v2": 0, "v3": 1}
FFN = ["fxt", "th", "sc", "h0", "h1", "h2", "h3", "ht0", "ht1", "ht2", "ht3", "w2"]
OUT = ["b0", "b1", "o", "ot"]
PREP = ["axt", "q", "k", "v0", "v1", "v2", "v3"]
FIRST_STEP, LOOP_STEP, NEXT_TO_LAST, LAST_STEP = FFN + PREP, FFN + OUT + PREP, FFN + OUT, FFN
SETUP = ["wq", "wk", "wv0", "wv1", "wo0", "wo1", "bias"]
SETUP_BANK = {"wq": 0, "wk": 1, "wv0": 0, "wv1": 1, "wo0": 0, "wo1": 1, "bias": 0}


def uses_before(name, t):
    if name in SETUP:
        b = SETUP_BANK[name]
        return b, sum(SETUP_BANK[n] == b for n in SETUP[:SETUP.index(name)])
    b = BANK[name]
    count = lambda names: sum(BANK[n] == b for n in names)
    n = sum(v == b for v in SETUP_BANK.values())
    if isinstance(t, int) and t == 0:
        return b, n + count(FIRST_STEP[:FIRST_STEP.index(name)])
    n += count(FIRST_STEP)
    if isinstance(t, int) and t == LAST:
        n += count(LOOP_STEP) * (NSEQ - 1) + count(NEXT_TO_LAST)
        return b, n + count(LAST_STEP[:LAST_STEP.index(name)])
    order = NEXT_TO_LAST if isinstance(t, int) and t == NSEQ else LOOP_STEP
    return b, (t - 1) * count(LOOP_STEP) + n + count(order[:order.index(name)])


def macaron(nc, x_d, wq_d, wk_d, wv_d, wo_d, mix_d, w1_d, b1_d, w2_d, b2_d, wo1_d, bo1_d, wo2_d, bo2_d,
            gamma_d, beta_d, out_d):
    with ExitStack() as ctx:
        def sb(name, shape, dt=F32):
            return ctx.enter_context(nc.sbuf_tensor(name, shape, dt))

        def ps(name, shape):
            return ctx.enter_context(nc.psum_tensor(name, shape, F32))

        def sem(name):
            return ctx.enter_context(nc.semaphore(name))

        ident = sb("ident", [P, P])
        causal = sb("causal", [P, P])
        head_row = sb("head_row", [P, NG, HALF])
        pick_row = sb("pick_row", [P, NG, P])
        minus_half = sb("minus_half", [P, SLAB])
        descending = sb("descending", [P, SLAB, PATHS])
        wq_in = sb("wq_in", [P, NT, D])
        wk_in = sb("wk_in", [P, NT, D])
        wv_in = sb("wv_in", [P, 8, D])
        wo_in = sb("wo_in", [P, HEADS * HD])
        wo_grouped = sb("wo_grouped", [P, NG, 2, GROUP, HALF])
        wqT = sb("wqT", [P, HEADS * FEAT])
        wkT = sb("wkT", [P, HEADS * FEAT])
        wvT = sb("wvT", [P, HEADS * HD])
        woT = sb("woT", [P, NG * 2, D])
        w1 = sb("w1", [P, PATHS, DM])
        wo1 = sb("wo1", [P, DM])
        wo2_diag = sb("wo2_diag", [P, SLAB * PATHS])
        w2 = sb("w2", [P, 3, D])
        w2_paths = sb("w2_paths", [3 * DM, 3, D])
        b1_diag = sb("b1_diag", [3 * DM, 3, PATHS])
        b2 = sb("b2", [PATHS, D])
        bo1 = sb("bo1", [P, 1])
        bo2 = sb("bo2", [P, SLAB, PATHS])
        mix = sb("mix", [P, 3])
        gamma = sb("gamma", [P, D])
        beta = sb("beta", [P, D])
        gamma_half = sb("gamma_half", [P, D])
        beta_half = sb("beta_half", [P, D])

        X = sb("X", [P, SLAB, D])
        stats = sb("stats", [P, SLAB, 6])
        moments = sb("moments", [P, SLAB, 2])
        rstd = sb("rstd", [P, SLAB])
        xn = sb("xn", [P, SLAB, D])
        xT = sb("xT", [P, NT, L + 2])
        xm = sb("xm", [P, NT, L])
        th = sb("th", [P, P])
        score = sb("score", [P, SLAB, PATHS])
        best = sb("best", [P, SLAB])
        hit = sb("hit", [P, SLAB, PATHS])
        hm = sb("hm", [P, SLAB, PATHS + HID])
        hT = sb("hT", [P, SLAB, 3 * P])
        z = sb("z", [P, SLAB, D])
        z_stats = sb("z_stats", [P, SLAB, 6])
        z_moments = sb("z_moments", [P, SLAB, 2])
        z_rstd = sb("z_rstd", [P, SLAB])
        zn = sb("zn", [P, SLAB, D])
        xb = sb("xb", [P, SLAB, D])
        x_new = sb("x_new", [P, SLAB, D])

        a_stats = sb("a_stats", [P, NT, 6])
        a_moments = sb("a_moments", [P, NT, 2])
        a_rstd = sb("a_rstd", [P, NT])
        xa = sb("xa", [P, NT, D])
        xaT = sb("xaT", [P, L])
        x_res = sb("x_res", [P, NT, D])
        parts = sb("parts", [P, 2, 3, 2 * L], BF16)
        rest = sb("rest", [P, 2, 2 * L])
        qs = sb("qs", [NSLOT * FEAT, HEADS, L], BF16)
        ks = sb("ks", [NSLOT * FEAT, HEADS, L], BF16)
        V = sb("V", [P, NT, HEADS * HD])
        A = [sb(f"A{i}", [P, 3, GROUP, P]) for i in range(2)]
        num = sb("num", [P, NG, 2, L])
        rden = sb("rden", [P, L])
        yT = sb("yT", [P, NG, 2, L])
        oT = sb("oT", [P, L])
        parts_dram = nc.dram_tensor("parts_dram", [2, 3, 2, P, L], BF16, kind="Internal").ap()

        S = ps("S", [P, 4, 512])
        N = ps("N", [P, 512])
        Dn = ps("Dn", [P, 512])
        G = [ps("G0", [P, 512]), ps("G1", [P, 512])]

        filled = [sem("bank0_filled"), sem("bank1_filled")]
        emptied = [sem("bank0_emptied"), sem("bank1_emptied")]
        weights_loaded = sem("weights_loaded")
        late_loaded = sem("late_loaded")
        const_ready = sem("const_ready")
        zeroed = sem("zeroed")
        wo_ready = sem("wo_ready")
        bo_half_ready = sem("bo_half_ready")
        x_loaded = sem("x_loaded")
        in_moments = sem("in_moments")
        in_rstd = sem("in_rstd")
        xn_ready = sem("xn_ready")
        xT_ready = sem("xT_ready")
        xm_ready = sem("xm_ready")
        th_ready = sem("th_ready")
        hm_ready = sem("hm_ready")
        hT_ready = sem("hT_ready")
        z_moments_ready = sem("z_moments_ready")
        z_rstd_ready = sem("z_rstd_ready")
        xb_ready = sem("xb_ready")
        x_new_ready = sem("x_new_ready")
        a_moments_ready = sem("a_moments_ready")
        a_rstd_ready = sem("a_rstd_ready")
        xa_ready = sem("xa_ready")
        xaT_ready = sem("xaT_ready")
        x_res_ready = sem("x_res_ready")
        part0_ready = sem("part0_ready")
        part1_ready = sem("part1_ready")
        part2_ready = sem("part2_ready")
        parts_stored = sem("parts_stored")
        stack_loaded = sem("stack_loaded")
        v_ready = sem("v_ready")
        s_filled = [sem("s01_filled"), sem("s23_filled")]
        squared = [sem("s01_squared"), sem("s23_squared")]
        diag_ready = sem("diag_ready")
        off_ready = sem("off_ready")
        av_done = sem("av_done")
        num_ready = sem("num_ready")
        rden_ready = sem("rden_ready")
        y_ready = sem("y_ready")
        oT_ready = sem("oT_ready")
        stored = sem("stored")
        dve_step = sem("dve_step")
        pool_step = sem("pool_step")

        def await_bank(pe, name, t=0):
            b, n = uses_before(name, t)
            if not (isinstance(n, int) and n == 0):
                pe.wait_ge(emptied[b], n)
            return G[b], filled[b]

        def await_filled(eng, name, t=0):
            b, n = uses_before(name, t)
            eng.wait_ge(filled[b], n + 1)
            return G[b], emptied[b]

        def wait_apart(eng, *waits):
            values = [v if isinstance(v, int) else eng.to_reg(v) for _, v in waits]
            eng.wait_ge(x_loaded, 16)
            for (signal, _), v in zip(waits, values):
                eng.wait_ge(signal, v)

        class Chain:

            def __init__(self, eng, sem, base=0):
                self.eng, self.sem, self.base, self.n = eng, sem, base, 0

            def mark(self, ins):
                ins.then_inc(self.sem, 1)
                self.n += 1

            def wait(self):
                self.eng.wait_ge(self.sem, self.base + self.n)

            def then(self, ins):
                self.mark(ins)
                self.wait()

        block = ctx.enter_context(nc.Block())

        @block.sync
        def _(sp):
            def load_x(t):
                sp.dma_start(X[:, 0:NT, :], x_d[t].rearrange("(n p) d -> p n d", p=P)).then_inc(x_loaded, 16)

            load_x(0)
            for dst, src in ((w1[:, :, :], w1_d.rearrange("p d m -> d p m")),
                             (wo1[:, :], wo1_d),
                             (mix[:, :], mix_d.rearrange("k d -> d k")),
                             (wq_in[:, :, :], wq_d.rearrange("(c p) d -> p c d", p=P)),
                             (wk_in[:, :, :], wk_d.rearrange("(c p) d -> p c d", p=P)),
                             (wv_in[:, :, :], wv_d.rearrange("(c p) d -> p c d", p=P)),
                             (wo_in[:, :], wo_d),
                             (bo2[:, :, :], bass.AP(bo2_d.tensor, 0, [[0, P], [0, SLAB], [1, PATHS]])),
                             (gamma[:, :], bass.AP(gamma_d.tensor, 0, [[0, P], [1, D]])),
                             (beta[:, :], bass.AP(beta_d.tensor, 0, [[0, P], [1, D]]))):
                sp.dma_start(dst, src, allow_slow_non_contiguous=True).then_inc(weights_loaded, 16)
            w2_rows = w2_d.rearrange("p m d -> (p m) d")
            b2_col = bo1_d.rearrange("(a b) -> a b", b=1)
            late = [(w2[PATHS:KCH, 0, :], w2_rows[0:KCH - PATHS, :]),
                    (w2[0:KCH, 1, :], w2_rows[KCH - PATHS:2 * KCH - PATHS, :]),
                    (w2[0:KCH, 2, :], w2_rows[2 * KCH - PATHS:3 * KCH - PATHS, :]),
                    (w2_paths[:, :, :], w2_rows.rearrange("(c r) d -> r c d", c=3)),
                    (b2[:, :], b2_d)]
            sp.wait_ge(zeroed, 1)
            for j in range(SLAB):
                late.append((bo1[DM * j:DM * (j + 1), :], b2_col))
                late.append((wo2_diag[DM * j:DM * (j + 1), PATHS * j:PATHS * (j + 1)], wo2_d))
            for p in range(PATHS):
                r = DM * (p % 3)
                late.append((b1_diag[r:r + DM, p // 3, p:p + 1], b1_d[p].rearrange("(a b) -> a b", b=1)))
            for dst, src in late:
                sp.dma_start(dst, src, allow_slow_non_contiguous=True).then_inc(late_loaded, 16)
            assert len(late) == N_LATE

            def load_next_x(t, seq):
                wait_apart(sp, (xn_ready, t + 1), (xb_ready, t + 1))
                load_x(seq)

            def store_out(t):
                wait_apart(sp, (x_new_ready, t + 1))
                sp.dma_start(out_d[t - 2].rearrange("(n p) d -> p n d", p=P),
                             x_new[:, NT:SLAB, :]).then_inc(stored, 16)

            def restack(t):
                for i, (stack, slots) in enumerate(((qs, QSLOT), (ks, KSLOT))):
                    sp.wait_ge(part2_ready, 2 * t + i + 1)
                    sp.wait_ge(part1_ready, 2 * t + i + 1)
                    sp.dma_start(parts_dram[i].rearrange("s c p t -> p s c t"),
                                 parts[:, i, :, :].rearrange("p s (c t) -> p s c t", c=2)).then_inc(parts_stored, 16)
                for i, (stack, slots) in enumerate(((qs, QSLOT), (ks, KSLOT))):
                    if i == 0:
                        wait_apart(sp, (parts_stored, 32 * t + 32))
                        if not (isinstance(t, int) and t == 0):
                            sp.wait_ge(s_filled[0], 4 * t)
                            sp.wait_ge(s_filled[1], 4 * t)
                    for j, s in enumerate(slots):
                        sp.dma_start(stack[FEAT * j:FEAT * (j + 1), :, :],
                                     parts_dram[i, s].rearrange("c (h f) t -> f (c h) t", f=FEAT))\
                          .then_inc(stack_loaded, 16)

            load_next_x(0, 1)
            restack(0)
            load_next_x(1, 2)
            restack(1)
            with sp.Fori(2, NSEQ - 1) as t:
                load_next_x(t, t + 1)
                store_out(t)
                sp.wait_ge(stored, 16 * (t - 1))
                restack(t)
            load_next_x(NSEQ - 1, NSEQ - 1)
            store_out(NSEQ - 1)
            restack(NSEQ - 1)
            load_next_x(NSEQ, NSEQ - 1)
            store_out(NSEQ)
            store_out(LAST)
            sp.wait_ge(stored, 16 * NSEQ)
            sp.wait_ge(stack_loaded, 16 * 2 * NSLOT * NSEQ)
            sp.wait_ge(parts_stored, 32 * NSEQ)

        @block.gpsimd
        def _(pool):
            link = Chain(pool, pool_step)
            link.mark(pool.memset(ident[:, :], 0.0))
            link.mark(pool.memset(causal[:, :], 1.0))
            link.mark(pool.memset(head_row[:, :, :], 0.0))
            link.mark(pool.memset(pick_row[:, :, :], 0.0))
            pool.memset(wo2_diag[:, :], 0.0)
            link.mark(pool.memset(b1_diag[:, :, :], 0.0))
            pool.memset(minus_half[:, :], -0.5)
            pool.memset(X[:, NT:SLAB, :], 0.0)
            pool.memset(xT[:, :, 0:1], 0.0)
            pool.memset(xT[:, :, L + 1:L + 2], 0.0)
            for p in range(PATHS):
                pool.memset(descending[:, :, p:p + 1], float(PATHS - p))
            link.wait()
            pool.memset(best[:, :], 0.0).then_inc(zeroed, 1)
            link.mark(pool.affine_select(out=ident[:, :], in_=ident[:, :], compare_op=ALU.not_equal, fill=1.0,
                                         base=0, pattern=[[-1, P]], channel_multiplier=1))
            link.mark(pool.affine_select(out=causal[:, :], in_=causal[:, :], compare_op=ALU.is_ge, fill=0.0,
                                         base=0, pattern=[[1, P]], channel_multiplier=-1))
            for g in range(NG):
                v = head_row[:, g, :].rearrange("p (a b) -> p a b", b=NG)[:, :, g:g + 1]
                link.mark(pool.memset(v, 1.0))
                for j in range(GROUP):
                    v = pick_row[:, g, HALF * j:HALF * (j + 1)]
                    link.mark(pool.affine_select(out=v, in_=v, compare_op=ALU.not_equal, fill=1.0,
                                                 base=-(HALF * j + g), pattern=[[0, HALF]],
                                                 channel_multiplier=1))
            link.wait()
            pool.memset(rest[:, 0, 0:1], 0.0).then_inc(const_ready, 1)

            def inverse_std(moments_t, rstd_t, ready, signal, t, n):
                wait_apart(pool, (ready, t + 1))
                link.then(pool.tensor_scalar(rstd_t[:, :], moments_t[:, :, 1], EPS_LN, 1.0, ALU.add, ALU.mult))
                pool.tensor_tensor(rstd_t[:, :], rstd_t[:, :], minus_half[:, 0:n], ALU.pow).then_inc(signal, 1)

            def residual(t):
                if isinstance(t, int) and t == 0:
                    pool.wait_ge(bo_half_ready, 1)
                else:
                    pool.wait_ge(x_new_ready, t)
                pool.wait_ge(x_loaded, 16 * t + 16)
                if not (isinstance(t, int) and t == 0):
                    pool.wait_ge(xn_ready, t + 1)
                pool.tensor_tensor(xb[:, :, :], X[:, :, :],
                                   beta_half[:, :].unsqueeze(1).to_broadcast([P, SLAB, D]),
                                   ALU.add).then_inc(xb_ready, 1)

            def off_diagonal(t, g):
                n = (t - 1) * NG + g + 1
                wait_apart(pool, (squared[0], n), (squared[1], n))
                a = A[g % 2][:, 2, :, :]
                pool.tensor_scalar(a, a, 1.0, 1.0, ALU.add, ALU.mult).then_inc(off_ready, 1)

            def keep_residual(t):
                waits = [(x_new_ready, t + 1)]
                if not (isinstance(t, int) and t == 0):
                    b, n = uses_before("ot", t)
                    waits.append((emptied[b], n + 1))
                wait_apart(pool, *waits)
                pool.tensor_scalar(x_res[:, :, :], x_new[:, 0:NT, :], 1.0, 1.0, ALU.mult, ALU.mult)\
                    .then_inc(x_res_ready, 1)

            def second_parts(t):
                for i in range(2):
                    b, n = uses_before("qk"[i], t)
                    waits = [(emptied[b], n + 1)]
                    if not (isinstance(t, int) and t == 0):
                        waits.append((parts_stored, 32 * t))
                    wait_apart(pool, *waits)
                    pool.tensor_scalar(parts[:, i, 1, :], rest[:, i, :], 1.0, 1.0, ALU.mult, ALU.mult)\
                        .then_inc(part1_ready, 1)

            def step(t, attend, prepare):
                inverse_std(moments, rstd, in_moments, in_rstd, t, SLAB)
                residual(t)
                if attend:
                    for g in range(NG):
                        off_diagonal(t, g)
                inverse_std(z_moments, z_rstd, z_moments_ready, z_rstd_ready, t, SLAB)
                if prepare:
                    inverse_std(a_moments, a_rstd, a_moments_ready, a_rstd_ready, t, NT)
                    keep_residual(t)
                    second_parts(t)

            link.base, link.n = link.n, 0
            step(0, False, True)
            link.base, link.n = link.base + link.n, 0
            first = link.base
            with pool.Fori(1, NSEQ) as t:
                link.base, link.n = (t - 1) * 3 + first, 0
                step(t, True, True)
                assert link.n == 3
            link.base, link.n = first + 3 * (NSEQ - 1), 0
            step(NSEQ, True, False)
            step(LAST, False, False)

        @block.scalar
        def _(act):
            copy = lambda out, src: act.activation(out, src, ACT.Copy)

            for name, dst in (("wq", wqT[:, :]), ("wv0", wvT[:, 0:512]), ("wo0", woT[:, 0:4, :])):
                g_, done = await_filled(act, name)
                src = g_[:, 0:256] if name == "wq" else g_[:, :]
                copy(dst, src if len(dst.shape) == 2 else src.rearrange("p (a b) -> p a b", b=P)).then_inc(done, 1)

            def transposed_slab(t):
                g_, done = await_filled(act, "fxt", t)
                if not (isinstance(t, int) and t == 0):
                    act.wait_ge(xm_ready, t)
                copy(xT[:, :, 1:L + 1], g_[:, :].rearrange("p (s t) -> p s t", s=NT)).then_inc(done, 1)

            def tanh(t):
                g_, done = await_filled(act, "th", t)
                if isinstance(t, int) and t == 0:
                    act.wait_ge(late_loaded, 16 * N_LATE)
                act.activation(th[:, :], g_[:, 0:P], ACT.Tanh, bias=bo1[:, 0:1]).then_inc(done, 1)

            def hidden_transposed(t, j):
                g_, done = await_filled(act, f"ht{j}", t)
                copy(hT[0:KCH, j, :], g_[0:KCH, 0:3 * P]).then_inc(done, 1)

            def square(t, g):
                n = (t - 1) * NG + g
                for p in range(2):
                    act.wait_ge(s_filled[p], n + 1)
                    if p == 0 and not (isinstance(n, int) and n < 2):
                        if isinstance(t, int) or g >= 2:
                            act.wait_ge(av_done, n - 1)
                        else:
                            act.wait_ge(num_ready, (t - 1) * NG)
                    act.activation(A[g % 2][:, :, 2 * p:2 * p + 2, :].rearrange("p b h q -> p h b q"),
                                   S[:, 2 * p:2 * p + 2, 0:3 * P].rearrange("p h (b q) -> p h b q", b=3),
                                   ACT.Square, bias=1.0, scale=0.25).then_inc(squared[p], 1)

            def take_num(t, g):
                act.wait_ge(av_done, (t - 1) * NG + g + 1)
                copy(num[:, g, :, :], N[:, :].rearrange("p (e q) -> p e q", e=2)).then_inc(num_ready, 1)

            def take_out(t):
                g_, done = await_filled(act, "o", t)
                copy(oT[:, :], g_[:, 0:L]).then_inc(done, 1)

            def prepare_seq(t):
                g_, done = await_filled(act, "axt", t)
                copy(xaT[:, :], g_[:, 0:L]).then_inc(done, 1)
                for i, name in enumerate("qk"):
                    g_, _ = await_filled(act, name, t)
                    if not (isinstance(t, int) and t == 0):
                        act.wait_ge(parts_stored, 32 * t)
                    copy(parts[:, i, 0, :], g_[:, :]).then_inc(part0_ready, 1)
                for i in range(4):
                    g_, done = await_filled(act, f"v{i}", t)
                    copy(V[:, i // 2, 512 * (i % 2):512 * (i % 2) + 512], g_[:, :]).then_inc(done, 1)

            def ffn_only(t):
                transposed_slab(t)
                tanh(t)
                for j in range(SLAB):
                    hidden_transposed(t, j)

            def attend_and_ffn(t):
                square(t, 0)
                transposed_slab(t)
                square(t, 1)
                take_num(t, 0)
                tanh(t)
                square(t, 2)
                take_num(t, 1)
                square(t, 3)
                take_num(t, 2)
                for j in range(SLAB):
                    hidden_transposed(t, j)
                take_num(t, 3)
                take_out(t)

            ffn_only(0)
            prepare_seq(0)
            with act.Fori(1, NSEQ) as t:
                attend_and_ffn(t)
                prepare_seq(t)
            attend_and_ffn(NSEQ)
            ffn_only(LAST)

        @block.vector
        def _(dve):
            link = Chain(dve, dve_step)

            dve.wait_ge(weights_loaded, 16 * N_WEIGHTS)
            heads = wo_in[:, :].rearrange("p (g j e f) -> p g e j f", g=NG, j=GROUP, e=2)
            for e in range(2):
                ins = dve.tensor_copy(wo_grouped[:, :, e], heads[:, :, e])
            ins.then_inc(wo_ready, 1)
            for name, dst in (("wk", wkT[:, :]), ("wv1", wvT[:, 512:1024]), ("wo1", woT[:, 4:8, :])):
                g_, done = await_filled(dve, name)
                src = g_[:, 0:256] if name == "wk" else g_[:, :]
                dve.tensor_copy(dst, src if len(dst.shape) == 2 else src.rearrange("p (a b) -> p a b", b=P))\
                    .then_inc(done, 1)
            dve.wait_ge(weights_loaded, 16 * N_WEIGHTS)
            link.mark(dve.tensor_scalar(gamma_half[:, :], gamma[:, :], 0.5, None, ALU.mult))
            dve.tensor_scalar(beta_half[:, :], beta[:, :], 0.5, None, ALU.mult).then_inc(bo_half_ready, 1)
            g_, done = await_filled(dve, "bias")
            dve.wait_ge(late_loaded, 16 * N_LATE)
            dve.tensor_tensor(w2[0:PATHS, 0, :], g_[0:PATHS, 0:D], b2[:, :], ALU.add).then_inc(done, 1)

            def statistics(src, st, mo, n, signal):
                for i in range(n):
                    ins = dve.bn_stats(st[:, i, :], src[:, i, :])
                link.mark(ins)
                wait_apart(dve, (link.sem, link.base + link.n))
                for i in range(n):
                    ins = dve.bn_aggr(mo[:, i, :], st[:, i, :])
                ins.then_inc(signal, 1)

            def normalise(dst, src, mo, rs, n):
                for i in range(n):
                    ins = dve.tensor_scalar(dst[:, i, :], src[:, i, :], mo[:, i, 0:1], rs[:, i:i + 1],
                                            ALU.subtract, ALU.mult)
                return ins

            def norm_in(t):
                dve.wait_ge(x_loaded, 16 * t + 16)
                if isinstance(t, int) and t == 0:
                    dve.wait_ge(const_ready, 1)
                else:
                    b, n = last_output(t)
                    dve.wait_ge(emptied[b], n)
                statistics(X, stats, moments, SLAB, in_moments)
                dve.wait_ge(in_rstd, t + 1)
                normalise(xn, X, moments, rstd, SLAB).then_inc(xn_ready, 1)

            def mix_tokens(t):
                b, n = uses_before("fxt", t)
                dve.wait_ge(emptied[b], n + 1)
                link.then(dve.tensor_scalar(xm[:, :, :], xT[:, :, 0:L], mix[:, 0:1], None, ALU.mult))
                link.then(dve.scalar_tensor_tensor(xm[:, :, :], xT[:, :, 1:L + 1], mix[:, 1:2], xm[:, :, :],
                                                   ALU.mult, ALU.add))
                dve.scalar_tensor_tensor(xm[:, :, :], xT[:, :, 2:L + 2], mix[:, 2:3], xm[:, :, :],
                                         ALU.mult, ALU.add).then_inc(xm_ready, 1)

            def choose_path(t):
                g_, done = await_filled(dve, "sc", t)
                dve.tensor_tensor(score[:, :, :], g_[:, 0:SLAB * PATHS].rearrange("p (a b) -> p a b", b=PATHS),
                                  bo2[:, :, :], ALU.add).then_inc(done, 1)
                dve.wait_ge(done, uses_before("sc", t)[1] + 1)
                link.then(dve.tensor_reduce(best[:, :], score[:, :, :], AX.X, ALU.max))
                wide = best[:, :].unsqueeze(2).to_broadcast([P, SLAB, PATHS])
                link.then(dve.tensor_tensor(hit[:, :, :], score[:, :, :], wide, ALU.is_ge))
                link.then(dve.tensor_tensor(hit[:, :, :], hit[:, :, :], descending[:, :, :], ALU.mult))
                link.then(dve.tensor_reduce(best[:, :], hit[:, :, :], AX.X, ALU.max))
                link.then(dve.tensor_tensor(hm[:, :, 0:PATHS], hit[:, :, :], wide, ALU.is_equal))

            def mask_hidden(t, j):
                g_, done = await_filled(dve, f"h{j}", t)
                dve.tensor_tensor(hm[:, j, PATHS:].rearrange("p (a b) -> p a b", b=DM),
                                  g_[:, 0:HID].rearrange("p (a b) -> p a b", b=DM),
                                  hm[:, j, 0:PATHS].unsqueeze(2).to_broadcast([P, PATHS, DM]),
                                  ALU.mult).then_inc(done, 1)

            def add_paths(t):
                g_, done = await_filled(dve, "w2", t)
                dve.tensor_tensor(z[:, :, :], g_[:, :].rearrange("p (a b) -> p a b", b=D), xn[:, :, :],
                                  ALU.add).then_inc(done, 1)
                dve.wait_ge(done, uses_before("w2", t)[1] + 1)
                statistics(z, z_stats, z_moments, SLAB, z_moments_ready)

            def norm_out(t):
                dve.wait_ge(z_rstd_ready, t + 1)
                link.then(normalise(zn, z, z_moments, z_rstd, SLAB))
                link.then(dve.tensor_tensor(zn[:, :, :], zn[:, :, :],
                                            gamma_half[:, :].unsqueeze(1).to_broadcast([P, SLAB, D]), ALU.mult))
                dve.wait_ge(xb_ready, t + 1)
                if not (isinstance(t, int) and t in (0, LAST)):
                    dve.wait_ge(x_res_ready, t)
                if isinstance(t, int) and t >= NSEQ:
                    dve.wait_ge(stored, 16 * (t - 2))
                dve.tensor_tensor(x_new[:, :, :], zn[:, :, :], xb[:, :, :], ALU.add).then_inc(x_new_ready, 1)

            def norm_seq_statistics(t):
                dve.wait_ge(x_new_ready, t + 1)
                statistics(x_new, a_stats, a_moments, NT, a_moments_ready)

            def norm_seq(t):
                dve.wait_ge(a_rstd_ready, t + 1)
                normalise(xa, x_new, a_moments, a_rstd, NT).then_inc(xa_ready, 1)

            def split_parts(t):
                for i, name in enumerate("qk"):
                    g_, done = await_filled(dve, name, t)
                    dve.wait_ge(part0_ready, 2 * t + i + 1)
                    dve.tensor_tensor(rest[:, i, :], g_[:, :], parts[:, i, 0, :], ALU.subtract)\
                        .then_inc(done, 1)
                for i in range(2):
                    dve.wait_ge(part1_ready, 2 * t + i + 1)
                    dve.tensor_tensor(parts[:, i, 2, :], rest[:, i, :], parts[:, i, 1, :], ALU.subtract)\
                        .then_inc(part2_ready, 1)

            def mask_diagonal(t, g):
                n = (t - 1) * NG + g + 1
                dve.wait_ge(squared[0], n)
                dve.wait_ge(squared[1], n)
                a = A[g % 2][:, 0:2, :, :].rearrange("p b h q -> p (b h) q")
                dve.scalar_tensor_tensor(a, a, 1.0, causal[:, :].unsqueeze(1).to_broadcast([P, 2 * GROUP, P]),
                                         ALU.add, ALU.mult).then_inc(diag_ready, 1)

            def invert_den(t):
                dve.wait_ge(av_done, (t - 1) * NG + NG)
                link.then(dve.tensor_scalar(rden[:, :], Dn[:, 0:L], 2 * EPS_DEN, None, ALU.add))
                dve.reciprocal(rden[:, :], rden[:, :]).then_inc(rden_ready, 1)

            def divide(t, i):
                g_, done = await_filled(dve, f"b{i}", t)
                dve.wait_ge(num_ready, (t - 1) * NG + 2 * i + 2)
                wide = g_[:, :].rearrange("p (g q) -> p g q", g=2).unsqueeze(2).to_broadcast([P, 2, 2, L])
                dve.tensor_tensor(yT[:, 2 * i:2 * i + 2, :, :], num[:, 2 * i:2 * i + 2, :, :], wide,
                                  ALU.mult).then_inc(done, 1)

            def add_attention(t):
                g_, done = await_filled(dve, "ot", t)
                dve.wait_ge(x_res_ready, t)
                dve.wait_ge(xb_ready, t + 1)
                dve.tensor_tensor(X[:, NT:SLAB, :], g_[:, 0:L].rearrange("p (a b) -> p a b", b=D),
                                  x_res[:, :, :], ALU.add).then_inc(done, 1)

            def ffn_only(t):
                norm_in(t)
                mix_tokens(t)
                choose_path(t)
                for j in range(SLAB):
                    mask_hidden(t, j)
                add_paths(t)
                norm_out(t)

            def attend_and_ffn(t):
                norm_in(t)
                mask_diagonal(t, 0)
                mix_tokens(t)
                mask_diagonal(t, 1)
                choose_path(t)
                mask_diagonal(t, 2)
                for j in range(SLAB):
                    mask_hidden(t, j)
                mask_diagonal(t, 3)
                invert_den(t)
                add_paths(t)
                divide(t, 0)
                divide(t, 1)
                norm_out(t)

            def prepare_seq(t):
                norm_seq_statistics(t)
                norm_seq(t)
                split_parts(t)

            ffn_only(0)
            prepare_seq(0)
            first = link.n
            with dve.Fori(1, NSEQ) as t:
                link.base, link.n = (t - 1) * DVE_STEPS + first, 0
                attend_and_ffn(t)
                norm_seq_statistics(t)
                add_attention(t)
                norm_seq(t)
                split_parts(t)
                assert link.n == DVE_STEPS, link.n
            link.base, link.n = first + DVE_STEPS * (NSEQ - 1), 0
            attend_and_ffn(NSEQ)
            add_attention(NSEQ)
            ffn_only(LAST)

        @block.tensor
        def _(pe):
            pe.wait_ge(const_ready, 1)
            pe.wait_ge(weights_loaded, 16 * N_WEIGHTS)

            def weights(name, sources):
                g_, done = await_bank(pe, name)
                for i, src in enumerate(sources):
                    mm = pe.transpose(g_[:, P * i:P * (i + 1)], src, ident[:, :])
                mm.then_inc(done, 1)

            wo_groups = wo_grouped[:, :, :, :, :].rearrange("p g e j f -> p g e (j f)")
            weights("wq", [wq_in[:, c, :] for c in range(2)])
            weights("wk", [wk_in[:, c, :] for c in range(2)])
            weights("wv0", [wv_in[:, c, :] for c in range(4)])
            weights("wv1", [wv_in[:, c, :] for c in range(4, 8)])
            pe.wait_ge(wo_ready, 1)
            weights("wo0", [wo_groups[:, c // 2, c % 2] for c in range(4)])
            weights("wo1", [wo_groups[:, c // 2, c % 2] for c in range(4, 8)])
            pe.wait_ge(late_loaded, 16 * N_LATE)
            g_, done = await_bank(pe, "bias")
            for c in range(3):
                mm = pe.matmul(g_[0:PATHS, 0:D], b1_diag[:, c, :], w2_paths[:, c, :], start=(c == 0),
                               stop=(c == 2))
            mm.then_inc(done, 1)

            def transpose_slab(t):
                pe.wait_ge(xn_ready, t + 1)
                g_, done = await_bank(pe, "fxt", t)
                for j in range(SLAB):
                    mm = pe.transpose(g_[:, P * j:P * (j + 1)], xn[:, j, :], ident[:, :])
                mm.then_inc(done, 1)

            xm_tiles = xm[:, :, :].rearrange("p s t -> p (s t)")

            def gate_hidden(t):
                pe.wait_ge(xm_ready, t + 1)
                g_, done = await_bank(pe, "th", t)
                for j in range(SLAB):
                    mm = pe.matmul(g_[DM * j:DM * (j + 1), 0:P], wo1[:, :], xm_tiles[:, P * j:P * (j + 1)],
                                   start=True, stop=True, skip_group_check=True)
                mm.then_inc(done, 1)

            def gate_scores(t):
                b, n = uses_before("th", t)
                pe.wait_ge(emptied[b], n + 1)
                g_, done = await_bank(pe, "sc", t)
                pe.matmul(g_[:, 0:SLAB * PATHS], th[:, :], wo2_diag[:, :], start=True, stop=True)\
                    .then_inc(done, 1)

            def path_hidden(t, j):
                g_, done = await_bank(pe, f"h{j}", t)
                pe.matmul(g_[:, 0:HID], xm_tiles[:, P * j:P * (j + 1)], w1[:, :, :].rearrange("p a b -> p (a b)"),
                          start=True, stop=True).then_inc(done, 1)

            def transpose_hidden(t, j):
                b, n = uses_before(f"h{j}", t)
                pe.wait_ge(emptied[b], n + 1)
                g_, done = await_bank(pe, f"ht{j}", t)
                for c in range(3):
                    mm = pe.transpose(g_[0:KCH, P * c:P * (c + 1)], hm[:, j, KCH * c:KCH * (c + 1)], ident[:, :])
                mm.then_inc(done, 1)

            def path_out(t):
                g_, done = await_bank(pe, "w2", t)
                for j in range(SLAB):
                    b, n = uses_before(f"ht{j}", t)
                    pe.wait_ge(emptied[b], n + 1)
                    for c in range(3):
                        mm = pe.matmul(g_[:, D * j:D * (j + 1)], hT[0:KCH, j, P * c:P * (c + 1)], w2[0:KCH, c, :],
                                       start=(c == 0), stop=(c == 2))
                mm.then_inc(done, 1)

            def scores(t, g):
                n = (t - 1) * NG + g
                if g == 0:
                    pe.wait_ge(stack_loaded, 16 * 2 * NSLOT * t)
                for p in range(2):
                    if not (isinstance(n, int) and n == 0):
                        pe.wait_ge(squared[p], n)
                    for h in (2 * p, 2 * p + 1):
                        head = GROUP * g + h
                        pe.matmul(S[:, h, 0:P], ks[:, head, P:L], qs[:, head, P:L], start=True, stop=True)
                        mm = pe.matmul(S[:, h, P:3 * P], ks[:, head, 0:P], qs[:, head, :], start=True, stop=True)
                    mm.then_inc(s_filled[p], 1)

            def values(t, g):
                n = (t - 1) * NG + g
                pe.wait_ge(diag_ready, n + 1)
                pe.wait_ge(off_ready, n + 1)
                if not (isinstance(n, int) and n == 0):
                    pe.wait_ge(num_ready, n)
                if g == 0:
                    if not (isinstance(t, int) and t == 1):
                        pe.wait_ge(rden_ready, t - 1)
                a = A[g % 2]
                for e in range(3):
                    for key in range(NT):
                        for j in range(GROUP):
                            rows = slice(HALF * j, HALF * (j + 1))
                            col = HD * (GROUP * g + j) + HALF * e
                            q0 = P * key
                            if e < 2:
                                out = N[rows, L * e + q0:L * (e + 1)]
                                lhsT = V[:, key, col:col + HALF]
                            else:
                                out = Dn[rows, q0:L]
                                lhsT = head_row[:, g, :]
                            rhs = a[:, 1:3, j, :] if key == 0 else a[:, 0, j, :]
                            first = key == 0 and (e < 2 or g == 0)
                            mm = pe.matmul(out, lhsT, rhs, start=first,
                                           stop=(key == 1 and (e < 2 or g == NG - 1)), skip_group_check=True)
                mm.then_inc(av_done, 1)

            def spread_den(t, i):
                pe.wait_ge(rden_ready, t)
                g_, done = await_bank(pe, f"b{i}", t)
                for k in range(2):
                    mm = pe.matmul(g_[:, L * k:L * (k + 1)], pick_row[:, 2 * i + k, :], rden[:, :], start=True,
                                   stop=True)
                mm.then_inc(done, 1)

            def project_out(t):
                g_, done = await_bank(pe, "o", t)
                for c in range(2 * NG):
                    if c % NG == 0:
                        b, n = uses_before(f"b{c // NG}", t)
                        pe.wait_ge(emptied[b], n + 1)
                    mm = pe.matmul(g_[:, 0:L], woT[:, c, :], yT[:, c // 2, c % 2, :], start=(c == 0),
                                   stop=(c == 2 * NG - 1))
                mm.then_inc(done, 1)

            def transpose_out(t):
                b, n = uses_before("o", t)
                pe.wait_ge(emptied[b], n + 1)
                g_, done = await_bank(pe, "ot", t)
                for i in range(NT):
                    mm = pe.transpose(g_[:, P * i:P * (i + 1)], oT[:, P * i:P * (i + 1)], ident[:, :])
                mm.then_inc(done, 1)

            def prepare_seq(t):
                pe.wait_ge(xa_ready, t + 1)
                g_, done = await_bank(pe, "axt", t)
                for i in range(NT):
                    mm = pe.transpose(g_[:, P * i:P * (i + 1)], xa[:, i, :], ident[:, :])
                mm.then_inc(done, 1)
                b, n = uses_before("axt", t)
                pe.wait_ge(emptied[b], n + 1)
                for name, w in (("q", wqT), ("k", wkT)):
                    g_, done = await_bank(pe, name, t)
                    for c in range(2):
                        mm = pe.matmul(g_[:, L * c:L * (c + 1)], w[:, P * c:P * (c + 1)], xaT[:, :], start=True,
                                       stop=True)
                    mm.then_inc(done, 1)
                for i in range(4):
                    g_, done = await_bank(pe, f"v{i}", t)
                    pe.matmul(g_[:, :], xaT[:, P * (i // 2):P * (i // 2 + 1)],
                              wvT[:, 512 * (i % 2):512 * (i % 2) + 512], start=True, stop=True).then_inc(done, 1)

            def ffn_only(t):
                transpose_slab(t)
                gate_hidden(t)
                gate_scores(t)
                for j in range(SLAB):
                    path_hidden(t, j)
                for j in range(SLAB):
                    transpose_hidden(t, j)
                path_out(t)

            def attend_and_ffn(t):
                scores(t, 0)
                transpose_slab(t)
                scores(t, 1)
                wait_values(t)
                values(t, 0)
                gate_hidden(t)
                gate_scores(t)
                scores(t, 2)
                values(t, 1)
                for j in range(SLAB):
                    path_hidden(t, j)
                scores(t, 3)
                values(t, 2)
                for j in range(SLAB):
                    transpose_hidden(t, j)
                values(t, 3)
                path_out(t)
                for i in range(2):
                    spread_den(t, i)
                project_out(t)
                transpose_out(t)

            def wait_values(t):
                for i in (2, 3):
                    b, n = uses_before_prev(f"v{i}", t)
                    pe.wait_ge(emptied[b], n + 1)

            ffn_only(0)
            prepare_seq(0)
            with pe.Fori(1, NSEQ) as t:
                attend_and_ffn(t)
                prepare_seq(t)
            attend_and_ffn(NSEQ)
            ffn_only(LAST)


N_WEIGHTS = 10
N_LATE = 5 + 2 * SLAB + PATHS
DVE_STEPS = 13


def uses_before_prev(name, t):
    b = BANK[name]
    count = lambda names: sum(BANK[n] == b for n in names)
    n = sum(v == b for v in SETUP_BANK.values()) + count(FIRST_STEP)
    n -= count(PREP[PREP.index(name):])
    return b, (t - 1) * count(LOOP_STEP) + n


def last_output(t):
    b = BANK["ot"]
    count = lambda names: sum(BANK[n] == b for n in names)
    n = sum(v == b for v in SETUP_BANK.values()) + count(FIRST_STEP)
    if isinstance(t, int) and t == LAST:
        return b, n + (NSEQ - 1) * count(LOOP_STEP) + count(NEXT_TO_LAST)
    return b, (t - 1) * count(LOOP_STEP) + n - count(LOOP_STEP) + count(LOOP_STEP[:LOOP_STEP.index("ot")]) + 1


_INS = ["L0_attn_hidden_states", "L0_attn_Wq", "L0_attn_Wk", "L0_attn_Wv", "L0_attn_Wo", "L0_ffn_mix_kernel",
        "L0_ffn_W1", "L0_ffn_b1", "L0_ffn_W2", "L0_ffn_b2", "L0_ffn_Wo1", "L0_ffn_bo1", "L0_ffn_Wo2",
        "L0_ffn_bo2", "L0_ffn_gamma", "L0_ffn_beta"]


def kernel(**inputs):
    import numpy as _np
    import concourse.bacc as _bacc
    from concourse import mybir as _mybir
    from concourse.bass_utils import run_bass_kernel_spmd as _run

    nc = _bacc.Bacc("TRN2", target_bir_lowering=False, num_devices=1)
    arrays, args = {}, []
    for name in _INS:
        a = _np.ascontiguousarray(inputs[name])
        arrays[f"in_{name}_dram"] = a
        args.append(nc.dram_tensor(f"in_{name}_dram", a.shape, _mybir.dt.from_np(a.dtype), kind="ExternalInput").ap())
    args.append(nc.dram_tensor("out_0_dram", (NSEQ, L, D), _mybir.dt.float32, kind="ExternalOutput").ap())
    macaron(nc, *args)
    r = _run(nc, [arrays], core_ids=[0])
    return r.results[0]["out_0_dram"]
```

```python
from contextlib import ExitStack

import concourse.bass as bass
from concourse import mybir

F32 = mybir.dt.float32
BF16 = mybir.dt.bfloat16
ALU = mybir.AluOpType
ACT = mybir.ActivationFunctionType
AX = mybir.AxisListType

P = 128
NSEQ, L, D = 8, 256, 128
NT = L // P
HEADS, FEAT, HD = 16, 16, 64
GROUP = 4
NG = HEADS // GROUP
HALF = HD // 2
PATHS, DM = 9, 32
HID = PATHS * DM
SLAB = 4
KCH = (PATHS + HID) // 3
QSLOT = (0, 0, 0, 1, 1, 2)
KSLOT = (0, 1, 2, 0, 1, 0)
NSLOT = len(QSLOT)
STACK_COUNT = 16 * 2 * NSLOT
EPS_LN = 1e-5
EPS_DEN = 1e-12
LAST = NSEQ + 2

FULL = ["fxt", "th", "v1", "sc", "v3", "h0", "h1", "h2", "h3", "ht0", "ht1", "ht2", "ht3", "b0", "b1",
        "w2", "o", "axt", "ot", "q", "k", "v0", "v2"]
ENDING = ["fxt", "th", "sc", "b0", "b1", "o", "h0", "ot", "h1", "ht0", "ht1", "w2"]
FIRST = ["fxt", "wq", "wk", "th", "sc", "h0", "h1", "wv0", "ht0", "ht1", "wv1", "bias", "w2", "wo0", "wo1",
         "axt", "q", "k", "v0", "v2"]
BANK = {"fxt": 0, "th": 1, "v1": 2, "sc": 0, "v3": 1, "h0": 2, "h1": 0, "h2": 1, "h3": 2,
        "ht0": 0, "ht1": 1, "ht2": 2, "ht3": 0, "b0": 1, "b1": 2, "w2": 0, "o": 1, "axt": 2, "ot": 0,
        "q": 1, "k": 2, "v0": 0, "v2": 1,
        "wq": 1, "wk": 2, "wv0": 1, "wv1": 0, "bias": 1, "wo0": 1, "wo1": 2}
NBANK = 3
FIRST_LOOP = 2


def ends(t):
    return not isinstance(t, int) or 2 <= t <= NSEQ + 1


def attends(t):
    return not isinstance(t, int) or 1 <= t <= NSEQ


def prepares(t):
    return not isinstance(t, int) or t < NSEQ


def tiles(t):
    if not isinstance(t, int) or FIRST_LOOP <= t < NSEQ:
        return slice(0, SLAB)
    return slice(NT, SLAB) if t in (NSEQ, LAST) else slice(0, NT)


def tile_range(t):
    return range(tiles(t).start, tiles(t).stop)


def order(t):
    if isinstance(t, int) and t == 0:
        return FIRST
    if isinstance(t, int) and t == NSEQ + 1:
        return ENDING
    dropped = [f"{h}{j}" for h in ("h", "ht") for j in range(SLAB) if j not in tile_range(t)]
    if not ends(t):
        dropped += ["b0", "b1", "o", "ot"]
    if not attends(t):
        dropped += ["v1", "v3"]
    if not prepares(t):
        dropped += ["axt", "q", "k", "v0", "v2"]
    return [n for n in FULL if n not in dropped]


def on_bank(names, b):
    return sum(BANK[n] == b for n in names)


def fills_before_step(b, t):
    n = 0
    for u in range(FIRST_LOOP if not isinstance(t, int) else t):
        n += on_bank(order(u), b)
    return n if isinstance(t, int) else (t - FIRST_LOOP) * on_bank(FULL, b) + n


def fills_before(name, t):
    b = BANK[name]
    return b, fills_before_step(b, t) + on_bank(order(t)[:order(t).index(name)], b)


def fills_through_last_out(t):
    b = BANK["ot"]
    return b, fills_before_step(b, t) - (0 if isinstance(t, int) and t > NSEQ else 1)


def macaron(nc, x_d, wq_d, wk_d, wv_d, wo_d, mix_d, w1_d, b1_d, w2_d, b2_d, wo1_d, bo1_d, wo2_d, bo2_d,
            gamma_d, beta_d, out_d):
    with ExitStack() as ctx:
        def sb(name, shape, dt=F32):
            return ctx.enter_context(nc.sbuf_tensor(name, shape, dt))

        def ps(name, shape):
            return ctx.enter_context(nc.psum_tensor(name, shape, F32))

        def sem(name):
            return ctx.enter_context(nc.semaphore(name))

        ident = sb("ident", [P, P])
        causal = sb("causal", [P, P])
        head_row = sb("head_row", [P, NG, HALF])
        pick_row = sb("pick_row", [P, NG, P])
        minus_half = sb("minus_half", [P, SLAB])
        eps = sb("eps", [P, 1])
        descending = sb("descending", [P, SLAB, PATHS])
        wq_in = sb("wq_in", [P, NT, D])
        wk_in = sb("wk_in", [P, NT, D])
        wv_in = sb("wv_in", [P, 8, D])
        wo_in = sb("wo_in", [P, 2, NG, GROUP * HALF])
        wqT = sb("wqT", [P, 2, FEAT, 8])
        wkT = sb("wkT", [P, 2, FEAT, 8])
        wvT = sb("wvT", [P, HEADS * HD])
        woT = sb("woT", [P, NG * 2, D])
        w1 = sb("w1", [P, PATHS, DM])
        wo1 = sb("wo1", [P, DM])
        wo2_rows = sb("wo2_rows", [P, PATHS])
        wo2_diag = sb("wo2_diag", [P, SLAB, PATHS])
        w2 = sb("w2", [P, 3, D])
        w2_paths = sb("w2_paths", [3 * DM, 3, D])
        b1_rows = sb("b1_rows", [3 * DM, 3])
        b1_diag = sb("b1_diag", [3 * DM, 3, PATHS])
        b2 = sb("b2", [PATHS, D])
        bo1 = sb("bo1", [P, 1])
        bo2 = sb("bo2", [P, SLAB, PATHS])
        mix = sb("mix", [P, 3])
        gamma = sb("gamma", [P, D])
        beta = sb("beta", [P, D])
        gamma_half = sb("gamma_half", [P, D])
        beta_half = sb("beta_half", [P, D])

        X = sb("X", [P, SLAB, D])
        stats = sb("stats", [P, SLAB, 6])
        moments = sb("moments", [P, SLAB, 2])
        rstd = sb("rstd", [P, SLAB])
        xn = sb("xn", [P, SLAB, D])
        xT = sb("xT", [P, NT, L + 2])
        xm = sb("xm", [P, NT, L])
        th = sb("th", [P, P])
        score = sb("score", [P, SLAB, PATHS])
        best = sb("best", [P, SLAB])
        hit = sb("hit", [P, SLAB, PATHS])
        hm = sb("hm", [P, SLAB, PATHS + HID])
        hT = sb("hT", [P, SLAB, 3 * P])
        z = sb("z", [P, SLAB, D])
        z_stats = sb("z_stats", [P, SLAB, 6])
        z_moments = sb("z_moments", [P, SLAB, 2])
        z_rstd = sb("z_rstd", [P, SLAB])
        zn = sb("zn", [P, SLAB, D])
        xb = sb("xb", [P, SLAB, D])
        x_new = sb("x_new", [P, SLAB, D])

        a_stats = sb("a_stats", [P, NT, 6])
        a_moments = sb("a_moments", [P, NT, 2])
        a_rstd = sb("a_rstd", [P, NT])
        xa = sb("xa", [P, NT, D])
        xaT = sb("xaT", [P, L])
        x_kept = sb("x_kept", [P, NT, D])
        x_res = sb("x_res", [P, NT, D])
        parts = sb("parts", [P, 2, 3, 2 * L], BF16)
        rest = sb("rest", [P, 2, 2 * L])
        qs = sb("qs", [NSLOT * FEAT, HEADS * L], BF16)
        ks = sb("ks", [NSLOT * FEAT, HEADS * L], BF16)
        V = sb("V", [P, NT, HEADS * HD])
        A = [sb(f"A{i}", [P, 3, GROUP, P]) for i in range(2)]
        num = sb("num", [P, NG, 2, L])
        den = sb("den", [P, L])
        rden = sb("rden", [P, L])
        yT = sb("yT", [P, NG, 2, L])
        oT = sb("oT", [P, L])

        S = ps("S", [P, 3, 512])
        N = ps("N", [P, 512])
        Dn = ps("Dn", [P, 512])
        G = [ps(f"G{i}", [P, 512]) for i in range(NBANK)]

        filled = [sem(f"bank{i}_filled") for i in range(NBANK)]
        emptied = [sem(f"bank{i}_emptied") for i in range(NBANK)]
        mix_loaded = sem("mix_loaded")
        ffn_loaded = sem("ffn_loaded")
        gate_loaded = sem("gate_loaded")
        w2_loaded = sem("w2_loaded")
        bias_loaded = sem("bias_loaded")
        scale_loaded = sem("scale_loaded")
        qkv_loaded = sem("qkv_loaded")
        wo_loaded = sem("wo_loaded")
        ident_ready = sem("ident_ready")
        zeros_ready = sem("zeros_ready")
        const_ready = sem("const_ready")
        diag_weights_ready = sem("diag_weights_ready")
        halves_ready = sem("halves_ready")
        x_loaded = sem("x_loaded")
        in_moments = sem("in_moments")
        in_rstd = sem("in_rstd")
        xn_ready = sem("xn_ready")
        xT_ready = sem("xT_ready")
        xm_ready = sem("xm_ready")
        th_ready = sem("th_ready")
        hm_ready = sem("hm_ready")
        hT_ready = sem("hT_ready")
        z_moments_ready = sem("z_moments_ready")
        z_rstd_ready = sem("z_rstd_ready")
        xb_ready = sem("xb_ready")
        x_new_ready = sem("x_new_ready")
        a_moments_ready = sem("a_moments_ready")
        a_rstd_ready = sem("a_rstd_ready")
        xa_ready = sem("xa_ready")
        xaT_ready = sem("xaT_ready")
        kept_ready = sem("kept_ready")
        x_res_ready = sem("x_res_ready")
        part_ready = [sem(f"part{i}_ready") for i in range(3)]
        stack_loaded = sem("stack_loaded")
        v_ready = sem("v_ready")
        s_filled = [sem("s01_filled"), sem("s23_filled")]
        squared = [sem("s01_squared"), sem("s23_squared")]
        diag_ready = sem("diag_ready")
        off_ready = sem("off_ready")
        av_done = sem("av_done")
        num_ready = sem("num_ready")
        den_ready = sem("den_ready")
        rden_ready = sem("rden_ready")
        y_ready = sem("y_ready")
        oT_ready = sem("oT_ready")
        stored = sem("stored")
        dve_step = sem("dve_step")
        pool_step = sem("pool_step")

        def await_bank(pe, name, t=0):
            b, n = fills_before(name, t)
            if not (isinstance(n, int) and n == 0):
                pe.wait_ge(emptied[b], n)
            return G[b], filled[b]

        def await_filled(eng, name, t=0):
            b, n = fills_before(name, t)
            eng.wait_ge(filled[b], n + 1)
            return G[b], emptied[b]

        def wait_apart(eng, *waits):
            values = [v if isinstance(v, int) else eng.to_reg(v) for _, v in waits]
            eng.wait_ge(x_loaded, 16)
            for (signal, _), v in zip(waits, values):
                eng.wait_ge(signal, v)

        def by_feature(bank):
            return bank[:, 0:HEADS * FEAT].rearrange("p (c r f) -> p c f r", c=2, r=8)

        class Chain:

            def __init__(self, eng, sem, base=0):
                self.eng, self.sem, self.base, self.n = eng, sem, base, 0

            def mark(self, ins):
                ins.then_inc(self.sem, 1)
                self.n += 1

            def wait(self):
                self.eng.wait_ge(self.sem, self.base + self.n)

            def then(self, ins):
                self.mark(ins)
                self.wait()

        block = ctx.enter_context(nc.Block())

        @block.sync
        def _(sp):
            def load_x(t):
                sp.dma_start(X[:, 0:NT, :], x_d[t].rearrange("(n p) d -> p n d", p=P)).then_inc(x_loaded, 16)

            load_x(0)
            sp.dma_start(mix[:, :], mix_d.rearrange("k d -> d k"), allow_slow_non_contiguous=True)\
              .then_inc(mix_loaded, 16)
            for dst, src in ((wo1[:, :], wo1_d),
                             (w1[:, :, :], w1_d.rearrange("p d m -> d p m"))):
                sp.dma_start(dst, src, allow_slow_non_contiguous=True).then_inc(ffn_loaded, 16)
            for dst, src in ((wq_in[:, :, :], wq_d.rearrange("(c p) d -> p c d", p=P)),
                             (wk_in[:, :, :], wk_d.rearrange("(c p) d -> p c d", p=P)),
                             (wv_in[:, :, :], wv_d.rearrange("(c p) d -> p c d", p=P))):
                sp.dma_start(dst, src).then_inc(qkv_loaded, 16)
            wo_heads = wo_d.rearrange("d (h e f) -> e d h f", h=HEADS, e=2)
            for e in range(2):
                sp.dma_start(wo_in[:, e, :, :].rearrange("p g (j f) -> p (g j) f", f=HALF), wo_heads[e])\
                  .then_inc(wo_loaded, 16)

            def load_next_x(t, seq):
                wait_apart(sp, (xn_ready, t + 1), (xb_ready, t + 1))
                load_x(seq)

            def store_out(t):
                wait_apart(sp, (x_new_ready, 2 * t + 2))
                sp.dma_start(out_d[t - 3].rearrange("(n p) d -> p n d", p=P),
                             x_new[:, NT:SLAB, :]).then_inc(stored, 16)

            def restack(t):
                if not (isinstance(t, int) and t == 0):
                    wait_apart(sp, (s_filled[0], 4 * t), (s_filled[1], 4 * t))
                for part in range(3):
                    for i, (stack, slots) in enumerate(((qs, QSLOT), (ks, KSLOT))):
                        sp.wait_ge(part_ready[part], 2 * t + i + 1)
                        for j in range(NSLOT):
                            if slots[j] == part:
                                sp.dma_start(stack[FEAT * j:FEAT * (j + 1), :].rearrange("f (r x) -> f r x", r=8),
                                             parts[:, i, part, :]).then_inc(stack_loaded, 16)

            load_next_x(0, 1)
            restack(0)
            load_next_x(1, 2)
            restack(1)
            load_next_x(2, 3)
            restack(2)
            with sp.Fori(3, NSEQ - 1) as t:
                load_next_x(t, t + 1)
                store_out(t)
                wait_apart(sp, (stored, 16 * (t - 2)))
                restack(t)
            load_next_x(NSEQ - 1, NSEQ - 1)
            store_out(NSEQ - 1)
            restack(NSEQ - 1)
            store_out(NSEQ)
            for t, half in ((LAST - 1, 0), (LAST, 1)):
                sp.wait_ge(x_new_ready, 2 * t + 1 + half)
                sp.dma_start(out_d[t - 3].rearrange("(n p) d -> p n d", p=P),
                             x_new[:, NT * half:NT * (half + 1), :]).then_inc(stored, 16)
            sp.wait_ge(stored, 16 * NSEQ)
            sp.wait_ge(stack_loaded, STACK_COUNT * NSEQ)

        @block.gpsimd
        def _(pool):
            link = Chain(pool, pool_step)

            def select(v, compare, fill, base, pattern, channel, signal=None):
                link.wait()
                ins = pool.affine_select(out=v, in_=v, compare_op=compare, fill=fill, base=base,
                                         pattern=pattern, channel_multiplier=channel)
                if signal is None:
                    link.mark(ins)
                else:
                    ins.then_inc(signal, 1)

            pool.memset(minus_half[:, :], -0.5)
            link.mark(pool.memset(ident[:, :], 0.0))
            select(ident[:, :], ALU.not_equal, 1.0, 0, [[-1, P]], 1, ident_ready)

            def inverse_std(moments_t, rstd_t, ready, signal, t, j):
                wait_apart(pool, (ready, t + 1))
                link.then(pool.tensor_scalar(rstd_t[:, j], moments_t[:, j, 1], EPS_LN, 1.0, ALU.add, ALU.mult))
                pool.tensor_tensor(rstd_t[:, j], rstd_t[:, j], minus_half[:, j], ALU.pow).then_inc(signal, 1)

            def constants():
                pool.memset(eps[:, :], 2 * EPS_DEN)
                pool.memset(xT[:, :, 0:1], 0.0)
                pool.memset(xT[:, :, L + 1:L + 2], 0.0)
                for p in range(PATHS):
                    pool.memset(descending[:, :, p:p + 1], float(PATHS - p))
                pool.memset(X[:, NT:SLAB, :], 0.0).then_inc(zeros_ready, 1)
                link.mark(pool.memset(wo2_diag[:, :, :], 1.0))
                select(wo2_diag[:, :, :], ALU.is_ge, 0.0, 0, [[-DM, SLAB], [0, PATHS]], 1)
                select(wo2_diag[:, :, :], ALU.is_ge, 0.0, DM - 1, [[DM, SLAB], [0, PATHS]], -1)
                link.mark(pool.memset(b1_diag[:, :, :], 1.0))
                select(b1_diag[:, :, :], ALU.is_ge, 0.0, 0, [[3 * DM, 3], [-DM, PATHS]], 1)
                select(b1_diag[:, :, :], ALU.is_ge, 0.0, DM - 1, [[-3 * DM, 3], [DM, PATHS]], -1)
                link.wait()
                pool.wait_ge(gate_loaded, 16 * 3)
                pool.tensor_tensor(wo2_diag[:, :, :], wo2_diag[:, :, :],
                                   wo2_rows[:, :].unsqueeze(1).to_broadcast([P, SLAB, PATHS]), ALU.mult)
                pool.wait_ge(bias_loaded, 16 * 3)
                pool.tensor_tensor(b1_diag[:, :, :], b1_diag[:, :, :],
                                   b1_rows[:, :].unsqueeze(2).to_broadcast([3 * DM, 3, PATHS]), ALU.mult)\
                    .then_inc(diag_weights_ready, 1)
                pool.wait_ge(scale_loaded, 16 * 2)
                pool.tensor_scalar(gamma_half[:, :], gamma[:, :], 0.5, 1.0, ALU.mult, ALU.mult)
                pool.tensor_scalar(beta_half[:, :], beta[:, :], 0.5, 1.0, ALU.mult, ALU.mult)\
                    .then_inc(halves_ready, 1)

            def attention_constants():
                link.mark(pool.memset(causal[:, :], 1.0))
                select(causal[:, :], ALU.is_ge, 0.0, 0, [[1, P]], -1)
                link.mark(pool.memset(head_row[:, :, :], 0.0))
                link.wait()
                for g in range(NG):
                    v = head_row[:, g, :].rearrange("p (a b) -> p a b", b=NG)[:, :, g:g + 1]
                    link.mark(pool.memset(v, 1.0))
                v = pick_row[:, :, :].rearrange("p g (j f) -> p g j f", f=HALF)
                link.mark(pool.memset(v, 0.0))
                select(v, ALU.not_equal, 1.0, 0, [[-1, NG], [-HALF, GROUP], [0, HALF]], 1, const_ready)

            def residual(t):
                j = tiles(t)
                if isinstance(t, int) and t == 0:
                    pool.wait_ge(halves_ready, 1)
                else:
                    pool.wait_ge(x_new_ready, 2 * t)
                pool.wait_ge(xn_ready, t + 1)
                pool.tensor_tensor(xb[:, j, :], X[:, j, :],
                                   beta_half[:, :].unsqueeze(1).to_broadcast([P, j.stop - j.start, D]),
                                   ALU.add).then_inc(xb_ready, 1)

            def off_diagonal(t, g):
                n = (t - 1) * NG + g + 2
                wait_apart(pool, (squared[0], n), (squared[1], n))
                a = A[g % 2][:, 2, :, :]
                pool.tensor_scalar(a, a, 1.0, 1.0, ALU.add, ALU.mult).then_inc(off_ready, 1)

            def keep_residuals(t):
                if ends(t):
                    if not (isinstance(t, int) and t == 2):
                        b, n = fills_through_last_out(t)
                        wait_apart(pool, (emptied[b], n))
                    link.then(pool.tensor_scalar(x_res[:, :, :], x_kept[:, :, :], 1.0, 1.0, ALU.mult, ALU.mult))
                    pool.sem_inc(x_res_ready, 1)
                if attends(t):
                    wait_apart(pool, (x_new_ready, 2 * t - 1))
                    pool.tensor_scalar(x_kept[:, :, :], x_new[:, 0:NT, :], 1.0, 1.0, ALU.mult, ALU.mult)\
                        .then_inc(kept_ready, 1)

            def second_parts(t):
                for i in range(2):
                    b, n = fills_before("qk"[i], t)
                    waits = [(emptied[b], n + 1)]
                    if not (isinstance(t, int) and t == 0):
                        waits.append((stack_loaded, STACK_COUNT * t))
                    wait_apart(pool, *waits)
                    pool.tensor_scalar(parts[:, i, 1, :], rest[:, i, :], 1.0, 1.0, ALU.mult, ALU.mult)\
                        .then_inc(part_ready[1], 1)

            def step(t):
                residual(t)
                keep_residuals(t)
                z_job = lambda: inverse_std(z_moments, z_rstd, z_moments_ready, z_rstd_ready, t, tiles(t))
                in_job = lambda: inverse_std(moments, rstd, in_moments, in_rstd, t + 1, tiles(t + 1))
                if isinstance(t, int) and t == NSEQ:
                    z_job()
                    in_job()
                    for g in range(NG):
                        off_diagonal(t, g)
                    return
                if isinstance(t, int) and t > NSEQ:
                    if t < LAST:
                        in_job()
                    z_job()
                    return
                if attends(t):
                    off_diagonal(t, 0)
                z_job()
                if attends(t):
                    off_diagonal(t, 1)
                inverse_std(a_moments, a_rstd, a_moments_ready, a_rstd_ready, t, slice(0, NT))
                if attends(t):
                    off_diagonal(t, 2)
                in_job()
                if attends(t):
                    off_diagonal(t, 3)
                second_parts(t)

            inverse_std(moments, rstd, in_moments, in_rstd, 0, tiles(0))
            constants()
            step(0)
            attention_constants()
            step(1)
            first = link.n
            with pool.Fori(FIRST_LOOP, NSEQ) as t:
                link.base, link.n = (t - FIRST_LOOP) * POOL_STEPS + first, 0
                step(t)
                assert link.n == POOL_STEPS
            link.base, link.n = first + POOL_STEPS * (NSEQ - FIRST_LOOP), 0
            for t in range(NSEQ, LAST + 1):
                step(t)

        @block.scalar
        def _(act):
            copy = lambda out, src: act.activation(out, src, ACT.Copy)

            w2_rows = w2_d.rearrange("p m d -> (p m) d")
            for dst, src, signal in (
                    (wo2_rows[:, :], bass.AP(wo2_d.tensor, 0, [[0, SLAB], [PATHS, DM], [1, PATHS]]), gate_loaded),
                    (bo1[:, :], bass.AP(bo1_d.tensor, 0, [[0, SLAB], [1, DM], [1, 1]]), gate_loaded),
                    (bo2[:, :, :], bass.AP(bo2_d.tensor, 0, [[0, P], [0, SLAB], [1, PATHS]]), gate_loaded),
                    (b1_rows[:, :], b1_d.rearrange("(c r) m -> (r m) c", c=3), bias_loaded),
                    (b2[:, :], b2_d, bias_loaded),
                    (w2_paths[:, :, :], w2_rows.rearrange("(c r) d -> r c d", c=3), bias_loaded),
                    (w2[PATHS:KCH, 0, :], w2_rows[0:KCH - PATHS, :], w2_loaded),
                    (w2[0:KCH, 1, :], w2_rows[KCH - PATHS:2 * KCH - PATHS, :], w2_loaded),
                    (w2[0:KCH, 2, :], w2_rows[2 * KCH - PATHS:3 * KCH - PATHS, :], w2_loaded),
                    (gamma[:, :], bass.AP(gamma_d.tensor, 0, [[0, P], [1, D]]), scale_loaded),
                    (beta[:, :], bass.AP(beta_d.tensor, 0, [[0, P], [1, D]]), scale_loaded)):
                act.dma_start(dst, src, allow_slow_non_contiguous=True).then_inc(signal, 16)

            def take_weights(*names):
                for name in names:
                    g_, done = await_filled(act, name)
                    src = g_[:, :]
                    if name in ("wq", "wk"):
                        dst, src = {"wq": wqT, "wk": wkT}[name][:, :, :, :], by_feature(g_)
                    elif name in ("wv0", "wv1"):
                        i = int(name[2])
                        dst = wvT[:, 512 * i:512 * i + 512]
                    else:
                        i = int(name[2])
                        dst, src = woT[:, 4 * i:4 * i + 4, :], src.rearrange("p (a b) -> p a b", b=P)
                    copy(dst, src).then_inc(done, 1)

            for signal in (squared[0], squared[1], num_ready, den_ready):
                act.sem_inc(signal, 1)

            def transposed_slab(t):
                g_, done = await_filled(act, "fxt", t)
                if not (isinstance(t, int) and t == 0):
                    act.wait_ge(xm_ready, t)
                else:
                    act.wait_ge(zeros_ready, 1)
                s = slice(tiles(t).start // NT, tiles(t).stop // NT)
                copy(xT[:, s, 1:L + 1], g_[:, :].rearrange("p (s t) -> p s t", s=NT)[:, s, :]).then_inc(done, 1)

            def tanh(t):
                g_, done = await_filled(act, "th", t)
                if isinstance(t, int) and t == 0:
                    act.wait_ge(gate_loaded, 16 * 3)
                rows = slice(DM * tiles(t).start, DM * tiles(t).stop)
                act.activation(th[rows, :], g_[rows, 0:P], ACT.Tanh, bias=bo1[rows, 0:1]).then_inc(done, 1)

            def hidden_transposed(t, j):
                g_, done = await_filled(act, f"ht{j}", t)
                copy(hT[0:KCH, j, :], g_[0:KCH, 0:3 * P]).then_inc(done, 1)

            def square(t, g):
                n = (t - 1) * NG + g
                a = A[g % 2]
                for p, (dst, src) in enumerate(((a[:, 0, :, :], S[:, 0, :].rearrange("p (h q) -> p h q", h=GROUP)),
                                                (a[:, 1:3, :, :].rearrange("p b h q -> p h b q"),
                                                 S[:, 1:3, :].rearrange("p s (h b q) -> p (s h) b q", h=2, b=2)))):
                    act.wait_ge(s_filled[p], n + 1)
                    if p == 0 and not (isinstance(n, int) and n < 2):
                        act.wait_ge(av_done, n - 1)
                    act.activation(dst, src, ACT.Square, bias=1.0, scale=0.25).then_inc(squared[p], 1)

            def take_num(seq, g):
                act.wait_ge(av_done, seq * NG + g + 1)
                copy(num[:, g, :, :], N[:, :].rearrange("p (e q) -> p e q", e=2)).then_inc(num_ready, 1)

            def take_den(seq):
                act.wait_ge(av_done, (seq + 1) * NG)
                act.activation(den[:, :], Dn[:, 0:L], ACT.Identity, bias=eps[:, 0:1]).then_inc(den_ready, 1)

            def take_out(t):
                g_, done = await_filled(act, "o", t)
                copy(oT[:, :], g_[:, 0:L]).then_inc(done, 1)

            def first_parts(t):
                for i, name in enumerate("qk"):
                    g_, _ = await_filled(act, name, t)
                    if not (isinstance(t, int) and t == 0):
                        act.wait_ge(stack_loaded, STACK_COUNT * t)
                    copy(parts[:, i, 0, :], g_[:, :]).then_inc(part_ready[0], 1)

            def take_value(t, i):
                g_, done = await_filled(act, f"v{i}", t)
                copy(V[:, i // 2, 512 * (i % 2):512 * (i % 2) + 512], g_[:, :]).then_inc(done, 1)

            def step(t):
                first = isinstance(t, int) and t == 0
                late = isinstance(t, int) and t >= NSEQ
                transposed_slab(t)
                if first:
                    take_weights("wq", "wk")
                if ends(t):
                    take_den(t - 2)
                tanh(t)
                if ends(t):
                    take_num(t - 2, 3)
                if attends(t):
                    take_value(t, 1)
                    take_value(t, 3)
                if first:
                    take_weights("wv0")
                if late and t == NSEQ + 1:
                    take_out(t)
                for j in tile_range(t):
                    hidden_transposed(t, j)
                if first:
                    take_weights("wv1", "wo0", "wo1")
                if late and t == NSEQ:
                    take_out(t)
                if attends(t):
                    square(t, 0)
                    square(t, 1)
                    take_num(t - 1, 0)
                    square(t, 2)
                if ends(t) and not late:
                    take_out(t)
                if attends(t):
                    take_num(t - 1, 1)
                if prepares(t):
                    g_, done = await_filled(act, "axt", t)
                    copy(xaT[:, :], g_[:, 0:L]).then_inc(done, 1)
                if attends(t):
                    square(t, 3)
                if prepares(t):
                    first_parts(t)
                if attends(t):
                    take_num(t - 1, 2)
                if prepares(t):
                    take_value(t, 0)
                    take_value(t, 2)

            step(0)
            step(1)
            with act.Fori(FIRST_LOOP, NSEQ) as t:
                step(t)
            for t in range(NSEQ, LAST + 1):
                step(t)

        @block.vector
        def _(dve):
            link = Chain(dve, dve_step)

            def statistics(src, st, mo, tiles, signal):
                for i in tiles:
                    ins = dve.bn_stats(st[:, i, :], src[:, i, :])
                link.mark(ins)
                wait_apart(dve, (link.sem, link.base + link.n))
                for i in tiles:
                    ins = dve.bn_aggr(mo[:, i, :], st[:, i, :])
                ins.then_inc(signal, 1)

            def normalise(dst, src, mo, rs, tiles):
                for i in tiles:
                    ins = dve.tensor_scalar(dst[:, i, :], src[:, i, :], mo[:, i, 0:1], rs[:, i:i + 1],
                                            ALU.subtract, ALU.mult)
                return ins

            def norm_in_statistics(t):
                if not (isinstance(t, int) and t > NSEQ):
                    dve.wait_ge(x_loaded, 16 * t + 16)
                if not isinstance(t, int) or t > FIRST_LOOP:
                    b, n = fills_before("ot", t - 1)
                    dve.wait_ge(emptied[b], n + 1)
                elif t == FIRST_LOOP:
                    dve.wait_ge(zeros_ready, 1)
                statistics(X, stats, moments, tile_range(t), in_moments)

            def norm_in(t):
                dve.wait_ge(in_rstd, t + 1)
                normalise(xn, X, moments, rstd, tile_range(t)).then_inc(xn_ready, 1)

            def mix_tokens(t):
                b, n = fills_before("fxt", t)
                dve.wait_ge(emptied[b], n + 1)
                if isinstance(t, int) and t == 0:
                    dve.wait_ge(mix_loaded, 16)
                s = slice(tiles(t).start // NT, tiles(t).stop // NT)
                link.then(dve.tensor_scalar(xm[:, s, :], xT[:, s, 0:L], mix[:, 0:1], None, ALU.mult))
                link.then(dve.scalar_tensor_tensor(xm[:, s, :], xT[:, s, 1:L + 1], mix[:, 1:2], xm[:, s, :],
                                                   ALU.mult, ALU.add))
                dve.scalar_tensor_tensor(xm[:, s, :], xT[:, s, 2:L + 2], mix[:, 2:3], xm[:, s, :],
                                         ALU.mult, ALU.add).then_inc(xm_ready, 1)

            def choose_path(t):
                g_, done = await_filled(dve, "sc", t)
                j = tiles(t)
                n = j.stop - j.start
                if isinstance(t, int) and t == 0:
                    dve.wait_ge(gate_loaded, 16 * 3)
                dve.tensor_tensor(score[:, j, :], g_[:, 0:n * PATHS].rearrange("p (a b) -> p a b", b=PATHS),
                                  bo2[:, j, :], ALU.add).then_inc(done, 1)
                dve.wait_ge(done, fills_before("sc", t)[1] + 1)
                link.then(dve.tensor_reduce(best[:, j], score[:, j, :], AX.X, ALU.max))
                wide = best[:, j].unsqueeze(2).to_broadcast([P, n, PATHS])
                link.then(dve.tensor_tensor(hit[:, j, :], score[:, j, :], wide, ALU.is_ge))
                link.then(dve.tensor_tensor(hit[:, j, :], hit[:, j, :], descending[:, j, :], ALU.mult))
                link.then(dve.tensor_reduce(best[:, j], hit[:, j, :], AX.X, ALU.max))
                link.then(dve.tensor_tensor(hm[:, j, 0:PATHS], hit[:, j, :], wide, ALU.is_equal))

            def bias_rows():
                g_, done = await_filled(dve, "bias")
                dve.tensor_tensor(w2[0:PATHS, 0, :], g_[0:PATHS, 0:D], b2[:, :], ALU.add).then_inc(done, 1)

            def mask_hidden(t, j):
                g_, done = await_filled(dve, f"h{j}", t)
                dve.tensor_tensor(hm[:, j, PATHS:].rearrange("p (a b) -> p a b", b=DM),
                                  g_[:, 0:HID].rearrange("p (a b) -> p a b", b=DM),
                                  hm[:, j, 0:PATHS].unsqueeze(2).to_broadcast([P, PATHS, DM]),
                                  ALU.mult).then_inc(done, 1)

            def add_paths(t):
                g_, done = await_filled(dve, "w2", t)
                j = tiles(t)
                dve.tensor_tensor(z[:, j, :], g_[:, :].rearrange("p (a b) -> p a b", b=D)[:, j, :], xn[:, j, :],
                                  ALU.add).then_inc(done, 1)
                dve.wait_ge(done, fills_before("w2", t)[1] + 1)
                statistics(z, z_stats, z_moments, tile_range(t), z_moments_ready)

            def norm_out(t):
                dve.wait_ge(z_rstd_ready, t + 1)
                link.mark(normalise(zn, z, z_moments, z_rstd, tile_range(t)))

            def scale_out(t, half):
                if NT * half not in tile_range(t):
                    dve.wait_ge(x_new_ready, 2 * t + half)
                    dve.sem_inc(x_new_ready, 1)
                    return
                j = slice(NT * half, NT * (half + 1))
                if j.start == tiles(t).start:
                    link.wait()
                if isinstance(t, int) and t == 0:
                    dve.wait_ge(halves_ready, 1)
                link.then(dve.tensor_tensor(zn[:, j, :], zn[:, j, :],
                                            gamma_half[:, :].unsqueeze(1).to_broadcast([P, NT, D]), ALU.mult))
                if j.start == tiles(t).start:
                    dve.wait_ge(xb_ready, t + 1)
                if half == 0 and not (isinstance(t, int) and t == 0):
                    dve.wait_ge(kept_ready, min(t, NSEQ) if isinstance(t, int) else t)
                if half == 1 and isinstance(t, int) and t >= NSEQ:
                    dve.wait_ge(stored, 16 * (NSEQ - 3 if t == NSEQ else NSEQ - 1))
                dve.tensor_tensor(x_new[:, j, :], zn[:, j, :], xb[:, j, :], ALU.add).then_inc(x_new_ready, 1)

            def norm_seq_statistics(t):
                dve.wait_ge(x_new_ready, 2 * t + 1)
                statistics(x_new, a_stats, a_moments, range(NT), a_moments_ready)

            def norm_seq(t):
                dve.wait_ge(a_rstd_ready, t + 1)
                normalise(xa, x_new, a_moments, a_rstd, range(NT)).then_inc(xa_ready, 1)

            def split_rest(t):
                for i, name in enumerate("qk"):
                    g_, done = await_filled(dve, name, t)
                    dve.wait_ge(part_ready[0], 2 * t + i + 1)
                    dve.tensor_tensor(rest[:, i, :], g_[:, :], parts[:, i, 0, :], ALU.subtract)\
                        .then_inc(done, 1)

            def third_parts(t):
                for i in range(2):
                    dve.wait_ge(part_ready[1], 2 * t + i + 1)
                    dve.tensor_tensor(parts[:, i, 2, :], rest[:, i, :], parts[:, i, 1, :], ALU.subtract)\
                        .then_inc(part_ready[2], 1)

            def mask_diagonal(t, g):
                n = (t - 1) * NG + g + 2
                if isinstance(n, int) and n == 2:
                    dve.wait_ge(const_ready, 1)
                dve.wait_ge(squared[0], n)
                dve.wait_ge(squared[1], n)
                a = A[g % 2][:, 0:2, :, :].rearrange("p b h q -> p (b h) q")
                dve.scalar_tensor_tensor(a, a, 1.0, causal[:, :].unsqueeze(1).to_broadcast([P, 2 * GROUP, P]),
                                         ALU.add, ALU.mult).then_inc(diag_ready, 1)

            def invert_den(seq):
                dve.wait_ge(den_ready, seq + 2)
                dve.reciprocal(rden[:, :], den[:, :]).then_inc(rden_ready, 1)

            def divide(t, i):
                g_, done = await_filled(dve, f"b{i}", t)
                dve.wait_ge(num_ready, (t - 2) * NG + 2 * i + 3)
                wide = g_[:, :].rearrange("p (g q) -> p g q", g=2).unsqueeze(2).to_broadcast([P, 2, 2, L])
                dve.tensor_tensor(yT[:, 2 * i:2 * i + 2, :, :], num[:, 2 * i:2 * i + 2, :, :], wide,
                                  ALU.mult).then_inc(done, 1)

            def add_attention(t):
                g_, done = await_filled(dve, "ot", t)
                dve.wait_ge(x_res_ready, t - 1)
                dve.wait_ge(xb_ready, t + 1)
                j = slice(NT, SLAB) if not isinstance(t, int) else tiles(t + 1) if t >= NSEQ else slice(NT, SLAB)
                dve.tensor_tensor(X[:, j, :], g_[:, 0:L].rearrange("p (a b) -> p a b", b=D),
                                  x_res[:, :, :], ALU.add).then_inc(done, 1)

            def step(t):
                mix_tokens(t)
                if isinstance(t, int) and t == NSEQ:
                    step_8(t)
                    return
                if isinstance(t, int) and t == NSEQ + 1:
                    step_9(t)
                    return
                choose_path(t)
                for j in tile_range(t):
                    mask_hidden(t, j)
                if isinstance(t, int) and t == 0:
                    bias_rows()
                if ends(t):
                    invert_den(t - 2)
                    divide(t, 0)
                    divide(t, 1)
                if attends(t):
                    mask_diagonal(t, 0)
                add_paths(t)
                if attends(t):
                    mask_diagonal(t, 1)
                norm_out(t)
                scale_out(t, 0)
                if prepares(t):
                    norm_seq_statistics(t)
                scale_out(t, 1)
                if prepares(t):
                    norm_seq(t)
                if attends(t):
                    mask_diagonal(t, 2)
                if ends(t):
                    add_attention(t)
                if prepares(t):
                    norm_in_statistics(t + 1)
                    split_rest(t)
                if attends(t):
                    mask_diagonal(t, 3)
                if prepares(t):
                    norm_in(t + 1)
                    third_parts(t)

            def step_8(t):
                choose_path(t)
                for j in tile_range(t):
                    mask_hidden(t, j)
                invert_den(t - 2)
                divide(t, 0)
                divide(t, 1)
                add_paths(t)
                norm_out(t)
                scale_out(t, 0)
                scale_out(t, 1)
                add_attention(t)
                norm_in_statistics(t + 1)
                mask_diagonal(t, 0)
                norm_in(t + 1)
                for g in range(1, NG):
                    mask_diagonal(t, g)

            def step_9(t):
                invert_den(t - 2)
                choose_path(t)
                divide(t, 0)
                divide(t, 1)
                mask_hidden(t, 0)
                add_attention(t)
                norm_in_statistics(t + 1)
                mask_hidden(t, 1)
                norm_in(t + 1)
                add_paths(t)
                norm_out(t)
                scale_out(t, 0)
                scale_out(t, 1)

            norm_in_statistics(0)
            norm_in(0)
            step(0)
            step(1)
            first = link.n
            with dve.Fori(FIRST_LOOP, NSEQ) as t:
                link.base, link.n = (t - FIRST_LOOP) * DVE_STEPS + first, 0
                step(t)
                assert link.n == DVE_STEPS, link.n
            link.base, link.n = first + DVE_STEPS * (NSEQ - FIRST_LOOP), 0
            for t in range(NSEQ, LAST + 1):
                step(t)

        @block.tensor
        def _(pe):
            pe.wait_ge(ident_ready, 1)

            def transpose_weights(*names):
                for name in names:
                    i = 4 * int(name[2]) if len(name) == 3 else 0
                    if name[1] == "o":
                        pe.wait_ge(wo_loaded, 16 * 2)
                        sources = [wo_in[:, c % 2, c // 2, :] for c in range(i, i + 4)]
                    else:
                        pe.wait_ge(qkv_loaded, 16 * 3)
                        sources = {"wq": [wq_in[:, c, :] for c in range(2)],
                                   "wk": [wk_in[:, c, :] for c in range(2)],
                                   "wv": [wv_in[:, c, :] for c in range(i, i + 4)]}[name[0:2]]
                    g_, done = await_bank(pe, name)
                    for c, src in enumerate(sources):
                        mm = pe.transpose(g_[:, P * c:P * (c + 1)], src, ident[:, :])
                    mm.then_inc(done, 1)

            def path_biases():
                pe.wait_ge(diag_weights_ready, 1)
                pe.wait_ge(bias_loaded, 16 * 3)
                g_, done = await_bank(pe, "bias")
                for c in range(3):
                    mm = pe.matmul(g_[0:PATHS, 0:D], b1_diag[:, c, :], w2_paths[:, c, :], start=(c == 0),
                                   stop=(c == 2))
                mm.then_inc(done, 1)

            def transpose_slab(t):
                pe.wait_ge(xn_ready, t + 1)
                g_, done = await_bank(pe, "fxt", t)
                for j in tile_range(t):
                    mm = pe.transpose(g_[:, P * j:P * (j + 1)], xn[:, j, :], ident[:, :])
                mm.then_inc(done, 1)

            xm_tiles = xm[:, :, :].rearrange("p s t -> p (s t)")

            def gate_hidden(t):
                if isinstance(t, int) and t == 0:
                    pe.wait_ge(ffn_loaded, 16 * 2)
                pe.wait_ge(xm_ready, t + 1)
                g_, done = await_bank(pe, "th", t)
                for j in tile_range(t):
                    mm = pe.matmul(g_[DM * j:DM * (j + 1), 0:P], wo1[:, :], xm_tiles[:, P * j:P * (j + 1)],
                                   start=True, stop=True, skip_group_check=True)
                mm.then_inc(done, 1)

            def gate_scores(t):
                b, n = fills_before("th", t)
                pe.wait_ge(emptied[b], n + 1)
                if isinstance(t, int) and t == 0:
                    pe.wait_ge(diag_weights_ready, 1)
                g_, done = await_bank(pe, "sc", t)
                j = tiles(t)
                rows = slice(DM * j.start, DM * j.stop)
                pe.matmul(g_[:, 0:PATHS * (j.stop - j.start)], th[rows, :],
                          wo2_diag[rows, j, :].rearrange("p j a -> p (j a)"), start=True, stop=True)\
                    .then_inc(done, 1)

            def path_hidden(t, j):
                g_, done = await_bank(pe, f"h{j}", t)
                pe.matmul(g_[:, 0:HID], xm_tiles[:, P * j:P * (j + 1)], w1[:, :, :].rearrange("p a b -> p (a b)"),
                          start=True, stop=True).then_inc(done, 1)

            def transpose_hidden(t, j):
                b, n = fills_before(f"h{j}", t)
                pe.wait_ge(emptied[b], n + 1)
                g_, done = await_bank(pe, f"ht{j}", t)
                for c in range(3):
                    mm = pe.transpose(g_[0:KCH, P * c:P * (c + 1)], hm[:, j, KCH * c:KCH * (c + 1)], ident[:, :])
                mm.then_inc(done, 1)

            def path_out(t):
                if isinstance(t, int) and t == 0:
                    b, n = fills_before("bias", 0)
                    pe.wait_ge(emptied[b], n + 1)
                    pe.wait_ge(w2_loaded, 16 * 3)
                g_, done = await_bank(pe, "w2", t)
                for j in tile_range(t):
                    b, n = fills_before(f"ht{j}", t)
                    pe.wait_ge(emptied[b], n + 1)
                    for c in range(3):
                        mm = pe.matmul(g_[:, D * j:D * (j + 1)], hT[0:KCH, j, P * c:P * (c + 1)], w2[0:KCH, c, :],
                                       start=(c == 0), stop=(c == 2))
                mm.then_inc(done, 1)

            def scores(t, g):
                n = (t - 1) * NG + g
                if g == 0:
                    pe.wait_ge(stack_loaded, STACK_COUNT * t)
                heads = [GROUP * g + h for h in range(GROUP)]
                at = [L * (2 * (head % 8) + head // 8) for head in heads]
                pe.wait_ge(squared[0], n + 1)
                for h, a in enumerate(at):
                    mm = pe.matmul(S[:, 0, P * h:P * (h + 1)], ks[:, a + P:a + L], qs[:, a + P:a + L],
                                   start=True, stop=True)
                mm.then_inc(s_filled[0], 1)
                pe.wait_ge(squared[1], n + 1)
                for h, a in enumerate(at):
                    mm = pe.matmul(S[:, 1 + h // 2, L * (h % 2):L * (h % 2 + 1)], ks[:, a:a + P], qs[:, a:a + L],
                                   start=True, stop=True)
                mm.then_inc(s_filled[1], 1)

            def values(seq, g):
                n = seq * NG + g
                if isinstance(n, int) and n == 0:
                    pe.wait_ge(const_ready, 1)
                pe.wait_ge(diag_ready, n + 1)
                pe.wait_ge(off_ready, n + 1)
                pe.wait_ge(num_ready, n + 1)
                if g == 0:
                    pe.wait_ge(den_ready, seq + 1)
                    for name in ("v0", "v2"):
                        b = BANK[name]
                        pe.wait_ge(emptied[b], fills_before_step(b, seq + 1))
                a = A[g % 2]
                for e in range(3):
                    for key in range(NT):
                        for j in range(GROUP):
                            rows = slice(HALF * j, HALF * (j + 1))
                            col = HD * (GROUP * g + j) + HALF * e
                            q0 = P * key
                            if e < 2:
                                out = N[rows, L * e + q0:L * (e + 1)]
                                lhsT = V[:, key, col:col + HALF]
                            else:
                                out = Dn[rows, q0:L]
                                lhsT = head_row[:, g, :]
                            rhs = a[:, 1:3, j, :] if key == 0 else a[:, 0, j, :]
                            first = key == 0 and (e < 2 or g == 0)
                            mm = pe.matmul(out, lhsT, rhs, start=first,
                                           stop=(key == 1 and (e < 2 or g == NG - 1)), skip_group_check=True)
                mm.then_inc(av_done, 1)

            def spread_den(t, i):
                pe.wait_ge(rden_ready, t - 1)
                g_, done = await_bank(pe, f"b{i}", t)
                for k in range(2):
                    mm = pe.matmul(g_[:, L * k:L * (k + 1)], pick_row[:, 2 * i + k, :], rden[:, :], start=True,
                                   stop=True)
                mm.then_inc(done, 1)

            def project_out(t):
                g_, done = await_bank(pe, "o", t)
                for c in range(2 * NG):
                    if c % NG == 0:
                        b, n = fills_before(f"b{c // NG}", t)
                        pe.wait_ge(emptied[b], n + 1)
                    mm = pe.matmul(g_[:, 0:L], woT[:, c, :], yT[:, c // 2, c % 2, :], start=(c == 0),
                                   stop=(c == 2 * NG - 1))
                mm.then_inc(done, 1)

            def transpose_out(t):
                b, n = fills_before("o", t)
                pe.wait_ge(emptied[b], n + 1)
                g_, done = await_bank(pe, "ot", t)
                for i in range(NT):
                    mm = pe.transpose(g_[:, P * i:P * (i + 1)], oT[:, P * i:P * (i + 1)], ident[:, :])
                mm.then_inc(done, 1)

            def transpose_seq(t):
                pe.wait_ge(xa_ready, t + 1)
                g_, done = await_bank(pe, "axt", t)
                for i in range(NT):
                    mm = pe.transpose(g_[:, P * i:P * (i + 1)], xa[:, i, :], ident[:, :])
                mm.then_inc(done, 1)

            def project_qk(t):
                b, n = fills_before("axt", t)
                pe.wait_ge(emptied[b], n + 1)
                for name, w in (("q", wqT), ("k", wkT)):
                    g_, done = await_bank(pe, name, t)
                    for c in range(2):
                        mm = pe.matmul(g_[:, L * c:L * (c + 1)], w[:, c, :, :].rearrange("p f r -> p (f r)"),
                                       xaT[:, :], start=True, stop=True)
                    mm.then_inc(done, 1)

            def project_v(t, i):
                g_, done = await_bank(pe, f"v{i}", t)
                pe.matmul(g_[:, :], xaT[:, P * (i // 2):P * (i // 2 + 1)],
                          wvT[:, 512 * (i % 2):512 * (i % 2) + 512], start=True, stop=True).then_inc(done, 1)

            def step(t):
                first = isinstance(t, int) and t == 0
                late = isinstance(t, int) and t == NSEQ
                transpose_slab(t)
                if first:
                    transpose_weights("wq", "wk")
                if ends(t):
                    values(t - 2, 3)
                gate_hidden(t)
                if attends(t):
                    project_v(t, 1)
                gate_scores(t)
                if isinstance(t, int) and t == NSEQ + 1:
                    step_9(t)
                    return
                if attends(t):
                    project_v(t, 3)
                for j in tile_range(t):
                    path_hidden(t, j)
                if first:
                    transpose_weights("wv0")
                for j in tile_range(t):
                    transpose_hidden(t, j)
                if first:
                    transpose_weights("wv1")
                    path_biases()
                if ends(t):
                    spread_den(t, 0)
                if attends(t) and not late:
                    scores(t, 0)
                if ends(t):
                    spread_den(t, 1)
                path_out(t)
                if first:
                    transpose_weights("wo0", "wo1")
                if late:
                    project_out(t)
                    scores(t, 0)
                    transpose_out(t)
                if attends(t):
                    scores(t, 1)
                    values(t - 1, 0)
                    scores(t, 2)
                if ends(t) and not late:
                    project_out(t)
                if attends(t):
                    values(t - 1, 1)
                if prepares(t):
                    transpose_seq(t)
                if ends(t) and not late:
                    transpose_out(t)
                if attends(t):
                    scores(t, 3)
                if prepares(t):
                    project_qk(t)
                if attends(t):
                    values(t - 1, 2)
                if prepares(t):
                    project_v(t, 0)
                    project_v(t, 2)

            def step_9(t):
                spread_den(t, 0)
                spread_den(t, 1)
                project_out(t)
                path_hidden(t, 0)
                transpose_out(t)
                path_hidden(t, 1)
                transpose_hidden(t, 0)
                transpose_hidden(t, 1)
                path_out(t)

            step(0)
            step(1)
            with pe.Fori(FIRST_LOOP, NSEQ) as t:
                step(t)
            for t in range(NSEQ, LAST + 1):
                step(t)


DVE_STEPS = 13
POOL_STEPS = 4


_INS = ["L0_attn_hidden_states", "L0_attn_Wq", "L0_attn_Wk", "L0_attn_Wv", "L0_attn_Wo", "L0_ffn_mix_kernel",
        "L0_ffn_W1", "L0_ffn_b1", "L0_ffn_W2", "L0_ffn_b2", "L0_ffn_Wo1", "L0_ffn_bo1", "L0_ffn_Wo2",
        "L0_ffn_bo2", "L0_ffn_gamma", "L0_ffn_beta"]


def kernel(**inputs):
    import numpy as _np
    import concourse.bacc as _bacc
    from concourse import mybir as _mybir
    from concourse.bass_utils import run_bass_kernel_spmd as _run

    nc = _bacc.Bacc("TRN2", target_bir_lowering=False, num_devices=1)
    arrays, args = {}, []
    for name in _INS:
        a = _np.ascontiguousarray(inputs[name])
        arrays[f"in_{name}_dram"] = a
        args.append(nc.dram_tensor(f"in_{name}_dram", a.shape, _mybir.dt.from_np(a.dtype), kind="ExternalInput").ap())
    args.append(nc.dram_tensor("out_0_dram", (NSEQ, L, D), _mybir.dt.float32, kind="ExternalOutput").ap())
    macaron(nc, *args)
    r = _run(nc, [arrays], core_ids=[0])
    return r.results[0]["out_0_dram"]
```

```python
from contextlib import ExitStack

import concourse.bass as bass
from concourse import mybir

F32 = mybir.dt.float32
BF16 = mybir.dt.bfloat16
ALU = mybir.AluOpType
ACT = mybir.ActivationFunctionType
AX = mybir.AxisListType

P = 128
NSEQ, L, D = 8, 256, 128
NT = L // P
HEADS, FEAT, HD = 16, 16, 64
GROUP = 4
NG = HEADS // GROUP
HALF = HD // 2
PATHS, DM = 9, 32
HID = PATHS * DM
LAST = NSEQ + 2
SLAB = 4
KCH = (PATHS + HID) // 3
QSLOT = (0, 0, 0, 1, 1, 2)
KSLOT = (0, 1, 2, 0, 1, 0)
NSLOT = len(QSLOT)
STACK_COUNT = 16 * 2 * NSLOT
EPS_LN = 1e-5
EPS_DEN = 1e-12

FULL = ["fxt", "v1", "th", "v3", "sc", "h0", "h1", "h2", "h3", "ht0", "ht1", "ht2", "ht3", "b0", "b1",
        "w2", "o", "axt", "q", "k", "v0", "v2"]
CLOSING = [(NSEQ, "o"), (NSEQ + 1, "b0"), (NSEQ + 1, "b1"), (NSEQ + 1, "o"), (NSEQ + 1, "fxt")] + \
    [(NSEQ + 1, n) for n in ("th", "h0", "sc", "h1")] + [(LAST, "fxt"), (NSEQ + 1, "ht0"), (NSEQ + 1, "ht1")] + \
    [(LAST, n) for n in ("th", "h2", "sc", "h3")] + [(NSEQ + 1, "w2")] + [(LAST, n) for n in ("ht2", "ht3", "w2")]
CLOSING_BANK = (1, 2, 0, 1, 2,
                0, 2, 1, 0, 1, 2, 0,
                1, 2, 0, 1, 0, 2, 1, 0)
FIRST = ["fxt", "th", "sc", "bias", "h0", "h1", "ht0", "ht1", "w2", "wq", "wk", "wv0", "wv1",
         "axt", "q", "k", "v0", "v2", "wo0", "wo1"]
BANK = {"fxt": 0, "v1": 1, "th": 2, "v3": 0, "sc": 1, "h0": 2, "h1": 0, "h2": 1, "h3": 2,
        "ht0": 0, "ht1": 1, "ht2": 2, "ht3": 0, "b0": 1, "b1": 2, "w2": 0, "o": 1, "axt": 2,
        "q": 0, "k": 1, "v0": 2, "v2": 1,
        "wq": 1, "wk": 2, "wv0": 0, "wv1": 1, "bias": 0, "wo0": 0, "wo1": 2}
NBANK = 3
FIRST_LOOP = 3
DVE_STEPS = 11
POOL_STEPS = 9


def in_loop(t):
    return not isinstance(t, int)


def ends(t):
    return not isinstance(t, int) or 2 <= t < LAST


def attends(t):
    return not isinstance(t, int) or 1 <= t <= NSEQ


def prepares(t):
    return not isinstance(t, int) or t < NSEQ


def tiles(t):
    if not isinstance(t, int) or FIRST_LOOP <= t < NSEQ:
        return slice(0, SLAB)
    return slice(NT, SLAB) if t in (NSEQ, LAST) else slice(0, NT)


def scaled_on_vector(t):
    return isinstance(t, int) and (t == 0 or t > NSEQ)


def tile_range(t):
    return range(tiles(t).start, tiles(t).stop)


def order(t):
    if isinstance(t, int) and t == 0:
        return FIRST
    dropped = [f"{h}{j}" for h in ("h", "ht") for j in range(SLAB) if j not in tile_range(t)]
    if not ends(t):
        dropped += ["b0", "b1"]
    if not ends(t) or (isinstance(t, int) and t == NSEQ):
        dropped += ["o"]
    if not attends(t):
        dropped += ["v1", "v3"]
    if not prepares(t):
        dropped += ["axt", "q", "k", "v0", "v2"]
    return [n for n in FULL if n not in dropped]


def on_bank(names, b):
    return sum(BANK[n] == b for n in names)


def fills_before_step(b, t):
    n = 0
    for u in range(FIRST_LOOP if not isinstance(t, int) else t):
        n += on_bank(order(u), b)
    return n if isinstance(t, int) else (t - FIRST_LOOP) * on_bank(FULL, b) + n


def fills_before(name, t):
    if isinstance(t, int) and (t, name) in CLOSING:
        i = CLOSING.index((t, name))
        b = CLOSING_BANK[i]
        return b, fills_before_step(b, NSEQ + 1) + CLOSING_BANK[:i].count(b)
    b = BANK[name]
    return b, fills_before_step(b, t) + on_bank(order(t)[:order(t).index(name)], b)


def fills_through_last_out(t):
    if isinstance(t, int):
        b, n = fills_before("o", t - 1)
        return b, n + 1
    b = BANK["o"]
    return b, fills_before_step(b, t) - on_bank(["axt", "q", "k", "v0", "v2"], b)


def macaron(nc, x_d, wq_d, wk_d, wv_d, wo_d, mix_d, w1_d, b1_d, w2_d, b2_d, wo1_d, bo1_d, wo2_d, bo2_d,
            gamma_d, beta_d, out_d):
    with ExitStack() as ctx:
        def sb(name, shape, dt=F32):
            return ctx.enter_context(nc.sbuf_tensor(name, shape, dt))

        def ps(name, shape):
            return ctx.enter_context(nc.psum_tensor(name, shape, F32))

        def sem(name):
            return ctx.enter_context(nc.semaphore(name))

        ident = sb("ident", [P, P])
        causal = sb("causal", [P, P])
        head_row = sb("head_row", [P, NG, HALF])
        pick_row = sb("pick_row", [P, NG, P], BF16)
        minus_after = sb("minus_after", [P, 2])
        minus_half = sb("minus_half", [P, SLAB])
        minus_one = sb("minus_one", [P, SLAB])
        eps = sb("eps", [P, 1])
        descending = sb("descending", [P, SLAB, PATHS])
        wq_in = sb("wq_in", [P, NT, D])
        wk_in = sb("wk_in", [P, NT, D])
        wv_in = sb("wv_in", [P, 8, D])
        wo_in = sb("wo_in", [P, 2, NG, GROUP * HALF])
        wqT = sb("wqT", [P, 2, FEAT, 8])
        wkT = sb("wkT", [P, 2, FEAT, 8])
        wvT = sb("wvT", [P, HEADS * HD])
        woT = sb("woT", [P, NG * 2, D])
        w1 = sb("w1", [P, PATHS, DM])
        wo1 = sb("wo1", [P, DM])
        wo2_rows = sb("wo2_rows", [P, PATHS])
        wo2_diag = sb("wo2_diag", [P, SLAB, PATHS])
        w2 = sb("w2", [P, 3, D])
        w2_paths = sb("w2_paths", [3 * DM, 3, D])
        b1_rows = sb("b1_rows", [3 * DM, 3])
        b1_diag = sb("b1_diag", [3 * DM, 3, PATHS])
        b2 = sb("b2", [PATHS, D])
        bo1 = sb("bo1", [P, 1])
        bo2 = sb("bo2", [P, SLAB, PATHS])
        mix = sb("mix", [P, 3])
        gamma = sb("gamma", [P, D])
        beta = sb("beta", [P, D])
        gamma_half = sb("gamma_half", [P, D])
        beta_half = sb("beta_half", [P, D])

        X = sb("X", [P, SLAB, D])
        stats = sb("stats", [P, SLAB, 6])
        moments = sb("moments", [P, SLAB, 2])
        rstd = sb("rstd", [P, SLAB])
        shift = sb("shift", [P, SLAB])
        xn = sb("xn", [P, SLAB, D])
        xT = sb("xT", [P, NT, L + 2])
        xm = sb("xm", [P, NT, L])
        th = sb("th", [P, P])
        score = sb("score", [P, SLAB, PATHS])
        best = sb("best", [P, SLAB])
        hit = sb("hit", [P, SLAB, PATHS])
        hm = sb("hm", [P, SLAB, PATHS + HID])
        hT = sb("hT", [P, SLAB, 3 * P])
        z = sb("z", [P, SLAB, D])
        z_stats = sb("z_stats", [P, SLAB, 6])
        z_moments = sb("z_moments", [P, SLAB, 2])
        z_rstd = sb("z_rstd", [P, SLAB])
        zn = sb("zn", [P, SLAB, D])
        xb = sb("xb", [P, SLAB, D])
        x_new = sb("x_new", [P, SLAB, D])

        a_stats = sb("a_stats", [P, NT, 6])
        a_moments = sb("a_moments", [P, NT, 2])
        a_rstd = sb("a_rstd", [P, NT])
        xa = sb("xa", [P, NT, D])
        xaT = sb("xaT", [P, L])
        x_kept = sb("x_kept", [P, NT, D])
        x_res = sb("x_res", [P, NT, D])
        parts = sb("parts", [P, 2, 3, 2 * L], BF16)
        rest = sb("rest", [P, 2, 2 * L])
        qs = sb("qs", [NSLOT * FEAT, HEADS * L], BF16)
        ks = sb("ks", [NSLOT * FEAT, HEADS * L], BF16)
        V = sb("V", [P, NT, HEADS * HD])
        A = [sb(f"A{i}", [P, 4, GROUP, P]) for i in range(2)]
        num = sb("num", [P, NG, 2, L])
        den = sb("den", [P, L])
        rden = sb("rden", [P, L])
        rden_high = sb("rden_high", [P, 2, L], BF16)
        rden_rest = sb("rden_rest", [P, L])
        rden_parts = sb("rden_parts", [P, L], BF16)
        yT = sb("yT", [P, NG, 2, L])

        S = ps("S", [P, 3, 512])
        N = ps("N", [P, 512])
        Dn = ps("Dn", [P, 512])
        G = [ps(f"G{i}", [P, 512]) for i in range(NBANK)]

        filled = [sem(f"bank{i}_filled") for i in range(NBANK)]
        emptied = [sem(f"bank{i}_emptied") for i in range(NBANK)]
        mix_loaded = sem("mix_loaded")
        ffn_loaded = sem("ffn_loaded")
        gate_loaded = sem("gate_loaded")
        w2_loaded = sem("w2_loaded")
        bias_loaded = sem("bias_loaded")
        scale_loaded = sem("scale_loaded")
        qkv_loaded = sem("qkv_loaded")
        wo_loaded = sem("wo_loaded")
        ident_ready = sem("ident_ready")
        zeros_ready = sem("zeros_ready")
        const_ready = sem("const_ready")
        diag_weights_ready = sem("diag_weights_ready")
        halves_ready = sem("halves_ready")
        x_loaded = sem("x_loaded")
        in_moments = sem("in_moments")
        in_rstd = sem("in_rstd")
        xn_ready = sem("xn_ready")
        xm_ready = sem("xm_ready")
        z_moments_ready = sem("z_moments_ready")
        z_rstd_ready = sem("z_rstd_ready")
        xb_ready = sem("xb_ready")
        x_new_ready = sem("x_new_ready")
        a_moments_ready = sem("a_moments_ready")
        a_rstd_ready = sem("a_rstd_ready")
        xa_ready = sem("xa_ready")
        kept_ready = sem("kept_ready")
        x_res_ready = sem("x_res_ready")
        part_ready = [sem(f"part{i}_ready") for i in range(3)]
        stack_loaded = sem("stack_loaded")
        s_filled = [sem("s01_filled"), sem("s23_filled")]
        squared = [sem("s01_squared"), sem("s23_squared")]
        diag_ready = sem("diag_ready")
        off_ready = sem("off_ready")
        sum_ready = sem("sum_ready")
        av_done = sem("av_done")
        num_ready = sem("num_ready")
        den_ready = sem("den_ready")
        rden_ready = sem("rden_ready")
        rden_parts_ready = sem("rden_parts_ready")
        stored = sem("stored")
        dve_step = sem("dve_step")
        pool_step = sem("pool_step")

        def await_bank(pe, name, t=0, known=False):
            b, n = fills_before(name, t)
            if not (isinstance(n, int) and n == 0) and not (known and in_loop(t)):
                pe.wait_ge(emptied[b], n)
            return G[b], filled[b]

        def await_filled(eng, name, t=0):
            b, n = fills_before(name, t)
            eng.wait_ge(filled[b], n + 1)
            return G[b], emptied[b]

        def wait_apart(eng, *waits):
            values = [v if isinstance(v, int) else eng.to_reg(v) for _, v in waits]
            eng.wait_ge(x_loaded, 16)
            for (signal, _), v in zip(waits, values):
                eng.wait_ge(signal, v)

        def by_feature(bank):
            return bank[:, 0:HEADS * FEAT].rearrange("p (c r f) -> p c f r", c=2, r=8)

        class Chain:

            def __init__(self, eng, sem, base=0):
                self.eng, self.sem, self.base, self.n = eng, sem, base, 0

            def mark(self, ins):
                ins.then_inc(self.sem, 1)
                self.n += 1

            def wait(self):
                self.eng.wait_ge(self.sem, self.base + self.n)

            def then(self, ins):
                self.mark(ins)
                self.wait()

        block = ctx.enter_context(nc.Block())

        @block.sync
        def _(sp):
            def load_x(t):
                sp.dma_start(X[:, 0:NT, :], x_d[t].rearrange("(n p) d -> p n d", p=P)).then_inc(x_loaded, 16)

            load_x(0)
            w2_rows = w2_d.rearrange("p m d -> (p m) d")
            wo_heads = wo_d.rearrange("d (h e f) -> e d h f", h=HEADS, e=2)
            for dst, src, signal in (
                    (mix[:, :], mix_d.rearrange("k d -> d k"), mix_loaded),
                    (wo1[:, :], wo1_d, ffn_loaded),
                    (w1[:, :, :], w1_d.rearrange("p d m -> d p m"), ffn_loaded),
                    (wo2_rows[:, :], bass.AP(wo2_d.tensor, 0, [[0, SLAB], [PATHS, DM], [1, PATHS]]), gate_loaded),
                    (bo1[:, :], bass.AP(bo1_d.tensor, 0, [[0, SLAB], [1, DM], [1, 1]]), gate_loaded),
                    (bo2[:, :, :], bass.AP(bo2_d.tensor, 0, [[0, P], [0, SLAB], [1, PATHS]]), gate_loaded),
                    (b1_rows[:, :], b1_d.rearrange("(c r) m -> (r m) c", c=3), bias_loaded),
                    (w2_paths[:, :, :], w2_rows.rearrange("(c r) d -> r c d", c=3), bias_loaded),
                    (b2[:, :], b2_d, bias_loaded),
                    (w2[PATHS:KCH, 0, :], w2_rows[0:KCH - PATHS, :], w2_loaded),
                    (w2[0:KCH, 1:3, :], w2_rows[KCH - PATHS:, :].rearrange("(c r) d -> r c d", c=2), w2_loaded),
                    (gamma[:, :], bass.AP(gamma_d.tensor, 0, [[0, P], [1, D]]), scale_loaded),
                    (beta[:, :], bass.AP(beta_d.tensor, 0, [[0, P], [1, D]]), scale_loaded),
                    (wq_in[:, :, :], wq_d.rearrange("(c p) d -> p c d", p=P), qkv_loaded),
                    (wk_in[:, :, :], wk_d.rearrange("(c p) d -> p c d", p=P), qkv_loaded),
                    (wv_in[:, :, :], wv_d.rearrange("(c p) d -> p c d", p=P), qkv_loaded)):
                sp.dma_start(dst, src, allow_slow_non_contiguous=True).then_inc(signal, 16)
            for e in range(2):
                sp.dma_start(wo_in[:, e, :, :].rearrange("p g (j f) -> p (g j) f", f=HALF), wo_heads[e])\
                  .then_inc(wo_loaded, 16)

            def load_next_x(t, seq):
                wait_apart(sp, (xn_ready, t + 1), (xb_ready, t + 1))
                load_x(seq)

            def store_out(t):
                wait_apart(sp, (x_new_ready, 2 * t + 2))
                sp.dma_start(out_d[t - 3].rearrange("(n p) d -> p n d", p=P),
                             x_new[:, NT:SLAB, :]).then_inc(stored, 16)

            def restack(t):
                if not (isinstance(t, int) and t == 0):
                    wait_apart(sp, (s_filled[0], 4 * t), (s_filled[1], 4 * t))
                for part in range(3):
                    for i, (stack, slots) in enumerate(((qs, QSLOT), (ks, KSLOT))):
                        sp.wait_ge(part_ready[part], 2 * t + i + 1)
                        for j in range(NSLOT):
                            if slots[j] == part:
                                sp.dma_start(stack[FEAT * j:FEAT * (j + 1), :].rearrange("f (r x) -> f r x", r=8),
                                             parts[:, i, part, :]).then_inc(stack_loaded, 16)

            load_next_x(0, 1)
            restack(0)
            load_next_x(1, 2)
            restack(1)
            load_next_x(2, 3)
            restack(2)
            with sp.Fori(3, NSEQ - 1) as t:
                load_next_x(t, t + 1)
                store_out(t)
                wait_apart(sp, (stored, 16 * (t - 2)))
                restack(t)
            load_next_x(NSEQ - 1, NSEQ - 1)
            store_out(NSEQ - 1)
            restack(NSEQ - 1)
            store_out(NSEQ)
            sp.wait_ge(stored, 16 * (NSEQ - 2))
            for t, half in ((LAST - 1, 0), (LAST, 1)):
                sp.wait_ge(x_new_ready, 2 * t + 1 + half)
                sp.dma_start(out_d[t - 3].rearrange("(n p) d -> p n d", p=P),
                             x_new[:, NT * half:NT * (half + 1), :]).then_inc(stored, 16)
            sp.wait_ge(stored, 16 * NSEQ)
            sp.wait_ge(stack_loaded, STACK_COUNT * NSEQ)

        @block.gpsimd
        def _(pool):
            link = Chain(pool, pool_step)

            def select(v, compare, fill, base, pattern, channel, signal=None):
                link.wait()
                ins = pool.affine_select(out=v, in_=v, compare_op=compare, fill=fill, base=base,
                                         pattern=pattern, channel_multiplier=channel)
                if signal is None:
                    link.mark(ins)
                else:
                    ins.then_inc(signal, 1)

            pool.memset(minus_half[:, :], -0.5)
            pool.memset(minus_one[:, :], -1.0)
            link.mark(pool.memset(ident[:, :], 0.0))
            select(ident[:, :], ALU.not_equal, 1.0, 0, [[-1, P]], 1, ident_ready)

            def inverse_std(moments_t, rstd_t, ready, signal, t, j):
                wait_apart(pool, (ready, t + 1))
                link.then(pool.tensor_scalar(rstd_t[:, j], moments_t[:, j, 1], EPS_LN, 1.0, ALU.add, ALU.mult))
                pool.tensor_tensor(rstd_t[:, j], rstd_t[:, j], minus_half[:, j], ALU.pow).then_inc(signal, 1)

            def input_scaling(t):
                j = tiles(t)
                if scaled_on_vector(t):
                    inverse_std(moments, rstd, in_moments, in_rstd, t, j)
                    return
                wait_apart(pool, (in_moments, t + 1))
                link.then(pool.tensor_scalar(rstd[:, j], moments[:, j, 1], EPS_LN, 1.0, ALU.add, ALU.mult))
                link.then(pool.tensor_tensor(rstd[:, j], rstd[:, j], minus_half[:, j], ALU.pow))
                link.then(pool.tensor_tensor(shift[:, j], rstd[:, j], moments[:, j, 0], ALU.mult))
                pool.tensor_tensor(shift[:, j], shift[:, j], minus_one[:, j], ALU.mult).then_inc(in_rstd, 1)

            def output_scaling(t):
                inverse_std(z_moments, z_rstd, z_moments_ready, z_rstd_ready, t, tiles(t))

            def constants():
                pool.memset(eps[:, :], 2 * EPS_DEN)
                pool.memset(xT[:, :, 0:1], 0.0)
                pool.memset(xT[:, :, L + 1:L + 2], 0.0)
                for p in range(PATHS - 1):
                    pool.memset(descending[:, :, p:p + 1], float(PATHS - p))
                pool.memset(descending[:, :, PATHS - 1:PATHS], 1.0).then_inc(zeros_ready, 1)
                link.mark(pool.memset(wo2_diag[:, :, :], 1.0))
                select(wo2_diag[:, :, :], ALU.is_ge, 0.0, 0, [[-DM, SLAB], [0, PATHS]], 1)
                select(wo2_diag[:, :, :], ALU.is_ge, 0.0, DM - 1, [[DM, SLAB], [0, PATHS]], -1)
                link.mark(pool.memset(b1_diag[:, :, :], 1.0))
                select(b1_diag[:, :, :], ALU.is_ge, 0.0, 0, [[3 * DM, 3], [-DM, PATHS]], 1)
                select(b1_diag[:, :, :], ALU.is_ge, 0.0, DM - 1, [[-3 * DM, 3], [DM, PATHS]], -1)
                link.wait()
                pool.wait_ge(gate_loaded, 16 * 3)
                pool.tensor_tensor(wo2_diag[:, :, :], wo2_diag[:, :, :],
                                   wo2_rows[:, :].unsqueeze(1).to_broadcast([P, SLAB, PATHS]), ALU.mult)
                pool.wait_ge(bias_loaded, 16 * 3)
                pool.tensor_tensor(b1_diag[:, :, :], b1_diag[:, :, :],
                                   b1_rows[:, :].unsqueeze(2).to_broadcast([3 * DM, 3, PATHS]), ALU.mult)\
                    .then_inc(diag_weights_ready, 1)
                pool.wait_ge(scale_loaded, 16 * 2)
                pool.tensor_scalar(gamma_half[:, :], gamma[:, :], 0.5, 1.0, ALU.mult, ALU.mult)
                pool.tensor_scalar(beta_half[:, :], beta[:, :], 0.5, 1.0, ALU.mult, ALU.mult)\
                    .then_inc(halves_ready, 1)

            def attention_constants():
                link.mark(pool.memset(causal[:, :], 1.0))
                select(causal[:, :], ALU.is_ge, 0.0, 0, [[1, P]], -1)
                link.mark(pool.memset(head_row[:, :, :], 0.0))
                link.wait()
                for g in range(NG):
                    v = head_row[:, g, :].rearrange("p (a b) -> p a b", b=NG)[:, :, g:g + 1]
                    link.mark(pool.memset(v, 1.0))
                link.then(pool.memset(minus_after[:, :], -1.0))
                for j in range(GROUP):
                    for c in range(2):
                        rows = slice(HALF * j, HALF * j + NG * (c + 1))
                        link.then(pool.memset(minus_after[rows, c:c + 1], 0.0))
                v = pick_row[:, :, :].rearrange("p g (j f) -> p g j f", f=HALF)
                link.mark(pool.memset(v, 0.0))
                for c in range(3):
                    select(v, ALU.not_equal, 1.0, -NG * c, [[-1, NG], [-HALF, GROUP], [0, HALF]], 1,
                           const_ready if c == 2 else None)

            def residual(t):
                j = tiles(t)
                if isinstance(t, int) and t == 0:
                    pool.wait_ge(halves_ready, 1)
                else:
                    pool.wait_ge(x_new_ready, 2 * NSEQ + 2 if isinstance(t, int) and t == LAST else 2 * t)
                pool.wait_ge(xn_ready, t + 1)
                pool.tensor_tensor(xb[:, j, :], X[:, j, :],
                                   beta_half[:, :].unsqueeze(1).to_broadcast([P, j.stop - j.start, D]),
                                   ALU.add).then_inc(xb_ready, 1)

            def off_diagonal(t, g):
                n = (t - 1) * NG + g + 2
                wait_apart(pool, (squared[0], n), (squared[1], n))
                a = A[g % 2][:, 2, :, :]
                pool.tensor_scalar(a, a, 1.0, 1.0, ALU.add, ALU.mult).then_inc(off_ready, 1)

            def sum_keys(t, g):
                n = (t - 1) * NG + g + 1
                pool.wait_ge(off_ready, n)
                pool.wait_ge(diag_ready, n)
                a = A[g % 2]
                pool.tensor_tensor(a[:, 3, :, :], a[:, 2, :, :], a[:, 0, :, :], ALU.add).then_inc(sum_ready, 1)

            def keep_residuals(t):
                if ends(t):
                    if not (isinstance(t, int) and t == 2):
                        b, n = fills_through_last_out(t)
                        wait_apart(pool, (emptied[b], n))
                    link.then(pool.tensor_scalar(x_res[:, :, :], x_kept[:, :, :], 1.0, 1.0, ALU.mult, ALU.mult))
                    pool.sem_inc(x_res_ready, 1)
                if attends(t):
                    wait_apart(pool, (x_new_ready, 2 * t - 1))
                    pool.tensor_scalar(x_kept[:, :, :], x_new[:, 0:NT, :], 1.0, 1.0, ALU.mult, ALU.mult)\
                        .then_inc(kept_ready, 1)

            def cut_inverse(seq):
                wait_apart(pool, (rden_ready, seq + 1))
                for i, (src, dst) in enumerate(((rden, rden_rest), (rden_rest, rden_parts))):
                    if i > 0:
                        wait_apart(pool, (link.sem, link.base + link.n))
                    link.then(pool.tensor_scalar(rden_high[:, i, :], src[:, :], minus_after[:, i:i + 1], 1.0,
                                                 ALU.mult, ALU.mult))
                    ins = pool.tensor_tensor(dst[:, :], src[:, :], rden_high[:, i, :], ALU.add)
                    if i == 0:
                        link.mark(ins)
                    else:
                        ins.then_inc(rden_parts_ready, 1)

            def second_parts(t):
                for i in range(2):
                    b, n = fills_before("qk"[i], t)
                    waits = [(emptied[b], n + 1)]
                    if not (isinstance(t, int) and t == 0):
                        waits.append((stack_loaded, STACK_COUNT * t))
                    wait_apart(pool, *waits)
                    pool.tensor_scalar(parts[:, i, 1, :], rest[:, i, :], 1.0, 1.0, ALU.mult, ALU.mult)\
                        .then_inc(part_ready[1], 1)

            def step(t):
                residual(t)
                if isinstance(t, int) and t == 0:
                    attention_constants()
                keep_residuals(t)
                if ends(t):
                    cut_inverse(t - 2)
                if attends(t):
                    off_diagonal(t, 0)
                    sum_keys(t, 0)
                output_scaling(t)
                if attends(t):
                    off_diagonal(t, 1)
                    sum_keys(t, 1)
                if prepares(t):
                    inverse_std(a_moments, a_rstd, a_moments_ready, a_rstd_ready, t, slice(0, NT))
                if attends(t):
                    off_diagonal(t, 2)
                    sum_keys(t, 2)
                if not (isinstance(t, int) and t == NSEQ):
                    input_scaling(t + 1)
                if attends(t):
                    off_diagonal(t, 3)
                if prepares(t):
                    second_parts(t)
                if attends(t):
                    sum_keys(t, 3)

            input_scaling(0)
            constants()
            step(0)
            for t in range(1, FIRST_LOOP):
                step(t)
            first = link.n
            with pool.Fori(FIRST_LOOP, NSEQ) as t:
                link.base, link.n = (t - FIRST_LOOP) * POOL_STEPS + first, 0
                step(t)
                assert link.n == POOL_STEPS
            link.base, link.n = first + POOL_STEPS * (NSEQ - FIRST_LOOP), 0
            step(NSEQ)
            input_scaling(NSEQ + 1)
            keep_residuals(NSEQ + 1)
            residual(NSEQ + 1)
            input_scaling(LAST)
            residual(LAST)
            output_scaling(NSEQ + 1)
            output_scaling(LAST)

        @block.scalar
        def _(act):
            def copy(out, src):
                return act.activation(out, src, ACT.Copy)

            def take_weights(*names):
                for name in names:
                    g_, done = await_filled(act, name)
                    src = g_[:, :]
                    if name in ("wq", "wk"):
                        dst, src = {"wq": wqT, "wk": wkT}[name][:, :, :, :], by_feature(g_)
                    elif name in ("wv0", "wv1"):
                        i = int(name[2])
                        dst = wvT[:, 512 * i:512 * i + 512]
                    else:
                        i = int(name[2])
                        dst, src = woT[:, 4 * i:4 * i + 4, :], src.rearrange("p (a b) -> p a b", b=P)
                    copy(dst, src).then_inc(done, 1)

            for signal in (squared[0], squared[1], num_ready, den_ready):
                act.sem_inc(signal, 1)

            def norm_in(t):
                act.wait_ge(in_rstd, t + 1)
                for j in tile_range(t):
                    ins = act.activation(xn[:, j, :], X[:, j, :], ACT.Identity, bias=shift[:, j:j + 1],
                                         scale=rstd[:, j:j + 1])
                ins.then_inc(xn_ready, 1)

            def transposed_slab(t):
                g_, done = await_filled(act, "fxt", t)
                if not (isinstance(t, int) and t == 0):
                    act.wait_ge(xm_ready, t)
                else:
                    act.wait_ge(zeros_ready, 1)
                s = slice(tiles(t).start // NT, tiles(t).stop // NT)
                copy(xT[:, s, 1:L + 1], g_[:, :].rearrange("p (s t) -> p s t", s=NT)[:, s, :]).then_inc(done, 1)

            def tanh(t):
                g_, done = await_filled(act, "th", t)
                if isinstance(t, int) and t == 0:
                    act.wait_ge(gate_loaded, 16 * 3)
                rows = slice(DM * tiles(t).start, DM * tiles(t).stop)
                act.activation(th[rows, :], g_[rows, 0:P], ACT.Tanh, bias=bo1[rows, 0:1]).then_inc(done, 1)

            def hidden_transposed(t, j):
                g_, done = await_filled(act, f"ht{j}", t)
                copy(hT[0:KCH, j, :], g_[0:KCH, 0:3 * P]).then_inc(done, 1)

            def square(t, g):
                n = (t - 1) * NG + g
                a = A[g % 2]
                for p, (dst, src) in enumerate(((a[:, 0, :, :], S[:, 0, :].rearrange("p (h q) -> p h q", h=GROUP)),
                                                (a[:, 1:3, :, :].rearrange("p b h q -> p h b q"),
                                                 S[:, 1:3, :].rearrange("p s (h b q) -> p (s h) b q", h=2, b=2)))):
                    act.wait_ge(s_filled[p], n + 1)
                    if p == 0 and not (isinstance(n, int) and n < 2):
                        act.wait_ge(av_done, n - 1)
                    act.activation(dst, src, ACT.Square, bias=1.0, scale=0.25).then_inc(squared[p], 1)

            def take_num(seq, g):
                act.wait_ge(av_done, seq * NG + g + 1)
                if g % 2 == 0 and ends(seq + 1):
                    b, n = fills_before(f"b{g // 2}", seq + 1)
                    act.wait_ge(emptied[b], n + 1)
                copy(num[:, g, :, :], N[:, :].rearrange("p (e q) -> p e q", e=2)).then_inc(num_ready, 1)

            def take_den(seq):
                act.wait_ge(av_done, (seq + 1) * NG)
                act.activation(den[:, :], Dn[:, 0:L], ACT.Identity, bias=eps[:, 0:1]).then_inc(den_ready, 1)

            def first_parts(t):
                for i, name in enumerate("qk"):
                    g_, _ = await_filled(act, name, t)
                    if not (isinstance(t, int) and t == 0):
                        act.wait_ge(stack_loaded, STACK_COUNT * t)
                    copy(parts[:, i, 0, :], g_[:, :]).then_inc(part_ready[0], 1)

            def take_value(t, i):
                g_, done = await_filled(act, f"v{i}", t)
                copy(V[:, i // 2, 512 * (i % 2):512 * (i % 2) + 512], g_[:, :]).then_inc(done, 1)

            def step(t):
                first = isinstance(t, int) and t == 0
                transposed_slab(t)
                if ends(t):
                    take_den(t - 2)
                if attends(t):
                    take_value(t, 1)
                tanh(t)
                if ends(t):
                    take_num(t - 2, 3)
                if attends(t):
                    take_value(t, 3)
                    square(t, 0)
                for j in tile_range(t):
                    hidden_transposed(t, j)
                if first:
                    take_weights("wq", "wk", "wv0", "wv1")
                if attends(t):
                    square(t, 1)
                    take_num(t - 1, 0)
                    square(t, 2)
                if prepares(t):
                    g_, done = await_filled(act, "axt", t)
                    copy(xaT[:, :], g_[:, 0:L]).then_inc(done, 1)
                if attends(t):
                    take_num(t - 1, 1)
                    square(t, 3)
                if prepares(t):
                    first_parts(t)
                if not scaled_on_vector(t + 1):
                    norm_in(t + 1)
                if prepares(t):
                    take_value(t, 0)
                if attends(t):
                    take_num(t - 1, 2)
                if prepares(t):
                    take_value(t, 2)
                if first:
                    take_weights("wo0", "wo1")

            step(0)
            for t in range(1, FIRST_LOOP):
                step(t)
            with act.Fori(FIRST_LOOP, NSEQ) as t:
                step(t)
            step(NSEQ)
            t = NSEQ + 1
            take_den(NSEQ - 1)
            take_num(NSEQ - 1, 3)
            transposed_slab(t)
            tanh(t)
            transposed_slab(LAST)
            hidden_transposed(t, 0)
            hidden_transposed(t, 1)
            tanh(LAST)
            hidden_transposed(LAST, 2)
            hidden_transposed(LAST, 3)

        @block.vector
        def _(dve):
            link = Chain(dve, dve_step)

            def statistics(src, st, mo, tiles, signal):
                for i in tiles:
                    ins = dve.bn_stats(st[:, i, :], src[:, i, :])
                link.mark(ins)
                wait_apart(dve, (link.sem, link.base + link.n))
                for i in tiles:
                    ins = dve.bn_aggr(mo[:, i, :], st[:, i, :])
                ins.then_inc(signal, 1)

            def normalise(dst, src, mo, rs, tiles):
                for i in tiles:
                    ins = dve.tensor_scalar(dst[:, i, :], src[:, i, :], mo[:, i, 0:1], rs[:, i:i + 1],
                                            ALU.subtract, ALU.mult)
                return ins

            def norm_in_statistics(t):
                if not (isinstance(t, int) and t > NSEQ):
                    dve.wait_ge(x_loaded, 16 * t + 16)
                if not isinstance(t, int) or t > 2:
                    b, n = fills_before("o", t - 1)
                    dve.wait_ge(emptied[b], n + 1)
                statistics(X, stats, moments, tile_range(t), in_moments)

            def norm_in(t):
                dve.wait_ge(in_rstd, t + 1)
                normalise(xn, X, moments, rstd, tile_range(t)).then_inc(xn_ready, 1)

            def mix_tokens(t):
                b, n = fills_before("fxt", t)
                dve.wait_ge(emptied[b], n + 1)
                if isinstance(t, int) and t == 0:
                    dve.wait_ge(mix_loaded, 16)
                s = slice(tiles(t).start // NT, tiles(t).stop // NT)
                link.then(dve.tensor_scalar(xm[:, s, :], xT[:, s, 0:L], mix[:, 0:1], None, ALU.mult))
                link.then(dve.scalar_tensor_tensor(xm[:, s, :], xT[:, s, 1:L + 1], mix[:, 1:2], xm[:, s, :],
                                                   ALU.mult, ALU.add))
                dve.scalar_tensor_tensor(xm[:, s, :], xT[:, s, 2:L + 2], mix[:, 2:3], xm[:, s, :],
                                         ALU.mult, ALU.add).then_inc(xm_ready, 1)

            def choose_path(t):
                g_, done = await_filled(dve, "sc", t)
                j = tiles(t)
                n = j.stop - j.start
                if isinstance(t, int) and t == 0:
                    dve.wait_ge(gate_loaded, 16 * 3)
                dve.tensor_tensor(score[:, j, :], g_[:, 0:n * PATHS].rearrange("p (a b) -> p a b", b=PATHS),
                                  bo2[:, j, :], ALU.add).then_inc(done, 1)
                dve.wait_ge(done, fills_before("sc", t)[1] + 1)
                link.then(dve.tensor_reduce(best[:, j], score[:, j, :], AX.X, ALU.max))
                wide = best[:, j].unsqueeze(2).to_broadcast([P, n, PATHS])
                link.then(dve.tensor_tensor(hit[:, j, :], score[:, j, :], wide, ALU.is_ge))
                link.then(dve.tensor_tensor(hit[:, j, :], hit[:, j, :], descending[:, j, :], ALU.mult))
                link.then(dve.tensor_reduce(best[:, j], hit[:, j, :], AX.X, ALU.max))
                link.then(dve.tensor_tensor(hm[:, j, 0:PATHS], hit[:, j, :], wide, ALU.is_equal))

            def bias_rows():
                g_, done = await_filled(dve, "bias")
                dve.tensor_tensor(w2[0:PATHS, 0, :], g_[0:PATHS, 0:D], b2[:, :], ALU.add).then_inc(done, 1)

            def mask_hidden(t, j):
                g_, done = await_filled(dve, f"h{j}", t)
                dve.tensor_tensor(hm[:, j, PATHS:].rearrange("p (a b) -> p a b", b=DM),
                                  g_[:, 0:HID].rearrange("p (a b) -> p a b", b=DM),
                                  hm[:, j, 0:PATHS].unsqueeze(2).to_broadcast([P, PATHS, DM]),
                                  ALU.mult).then_inc(done, 1)

            def add_paths(t):
                g_, done = await_filled(dve, "w2", t)
                j = tiles(t)
                dve.tensor_tensor(z[:, j, :], g_[:, :].rearrange("p (a b) -> p a b", b=D)[:, j, :], xn[:, j, :],
                                  ALU.add).then_inc(done, 1)
                dve.wait_ge(done, fills_before("w2", t)[1] + 1)
                statistics(z, z_stats, z_moments, tile_range(t), z_moments_ready)

            def centre_out(t):
                if isinstance(t, int) and t == 0:
                    dve.wait_ge(halves_ready, 1)
                dve.wait_ge(z_moments_ready, t + 1)
                for j in tile_range(t):
                    ins = dve.scalar_tensor_tensor(zn[:, j, :], z[:, j, :], z_moments[:, j, 0:1], gamma_half[:, :],
                                                   ALU.subtract, ALU.mult)
                link.mark(ins)

            def scale_out(t, half):
                if NT * half not in tile_range(t):
                    dve.wait_ge(x_new_ready, 2 * t + half)
                    dve.sem_inc(x_new_ready, 1)
                    return
                j = slice(NT * half, NT * (half + 1))
                if j.start == tiles(t).start:
                    link.wait()
                    dve.wait_ge(z_rstd_ready, t + 1)
                    dve.wait_ge(xb_ready, t + 1)
                if half == 0 and not (isinstance(t, int) and t == 0):
                    dve.wait_ge(kept_ready, min(t, NSEQ) if isinstance(t, int) else t)
                if half == 1 and isinstance(t, int) and t >= NSEQ:
                    dve.wait_ge(stored, 16 * (NSEQ - 3 if t == NSEQ else NSEQ - 2))
                for i in range(j.start, j.stop):
                    ins = dve.scalar_tensor_tensor(x_new[:, i, :], zn[:, i, :], z_rstd[:, i:i + 1], xb[:, i, :],
                                                   ALU.mult, ALU.add)
                ins.then_inc(x_new_ready, 1)

            def norm_seq_statistics(t):
                dve.wait_ge(x_new_ready, 2 * t + 1)
                statistics(x_new, a_stats, a_moments, range(NT), a_moments_ready)

            def norm_seq(t):
                dve.wait_ge(a_rstd_ready, t + 1)
                normalise(xa, x_new, a_moments, a_rstd, range(NT)).then_inc(xa_ready, 1)

            def split_rest(t):
                for i, name in enumerate("qk"):
                    g_, done = await_filled(dve, name, t)
                    dve.wait_ge(part_ready[0], 2 * t + i + 1)
                    dve.tensor_tensor(rest[:, i, :], g_[:, :], parts[:, i, 0, :], ALU.subtract)\
                        .then_inc(done, 1)

            def third_parts(t):
                for i in range(2):
                    dve.wait_ge(part_ready[1], 2 * t + i + 1)
                    dve.tensor_tensor(parts[:, i, 2, :], rest[:, i, :], parts[:, i, 1, :], ALU.subtract)\
                        .then_inc(part_ready[2], 1)

            def mask_diagonal(t, g):
                n = (t - 1) * NG + g + 2
                if isinstance(n, int) and n == 2:
                    dve.wait_ge(const_ready, 1)
                dve.wait_ge(squared[0], n)
                dve.wait_ge(squared[1], n)
                a = A[g % 2][:, 0:2, :, :].rearrange("p b h q -> p (b h) q")
                dve.scalar_tensor_tensor(a, a, 1.0, causal[:, :].unsqueeze(1).to_broadcast([P, 2 * GROUP, P]),
                                         ALU.add, ALU.mult).then_inc(diag_ready, 1)

            def invert_den(seq):
                dve.wait_ge(den_ready, seq + 2)
                dve.reciprocal(rden[:, :], den[:, :]).then_inc(rden_ready, 1)

            def cut_last_inverse():
                dve.wait_ge(rden_ready, NSEQ)
                for i, (src, dst) in enumerate(((rden, rden_rest), (rden_rest, rden_parts))):
                    link.then(dve.tensor_scalar(rden_high[:, i, :], src[:, :], minus_after[:, i:i + 1], None,
                                                ALU.mult))
                    ins = dve.tensor_tensor(dst[:, :], src[:, :], rden_high[:, i, :], ALU.add)
                    if i == 0:
                        link.then(ins)
                    else:
                        ins.then_inc(rden_parts_ready, 1)

            def divide(t, i):
                g_, done = await_filled(dve, f"b{i}", t)
                dve.wait_ge(num_ready, (t - 2) * NG + 2 * i + 3)
                wide = g_[:, :].rearrange("p (g q) -> p g q", g=2).unsqueeze(2).to_broadcast([P, 2, 2, L])
                dve.tensor_tensor(yT[:, 2 * i:2 * i + 2, :, :], num[:, 2 * i:2 * i + 2, :, :], wide,
                                  ALU.mult).then_inc(done, 1)

            def add_attention(t):
                g_, done = await_filled(dve, "o", t)
                dve.wait_ge(x_res_ready, t - 1)
                dve.wait_ge(xb_ready, t + 1)
                j = slice(0, NT) if isinstance(t, int) and t == NSEQ else slice(NT, SLAB)
                dve.tensor_tensor(X[:, j, :], g_[:, 0:L].rearrange("p (a b) -> p a b", b=D),
                                  x_res[:, :, :], ALU.add).then_inc(done, 1)

            def step(t):
                mix_tokens(t)
                if ends(t):
                    invert_den(t - 2)
                choose_path(t)
                if isinstance(t, int) and t == 0:
                    bias_rows()
                for j in tile_range(t):
                    mask_hidden(t, j)
                if attends(t):
                    mask_diagonal(t, 0)
                if ends(t):
                    divide(t, 0)
                    divide(t, 1)
                add_paths(t)
                centre_out(t)
                if attends(t):
                    mask_diagonal(t, 1)
                scale_out(t, 0)
                if prepares(t):
                    norm_seq_statistics(t)
                scale_out(t, 1)
                if prepares(t):
                    norm_seq(t)
                if attends(t):
                    mask_diagonal(t, 2)
                if not (isinstance(t, int) and t == NSEQ):
                    if ends(t):
                        add_attention(t)
                    norm_in_statistics(t + 1)
                if prepares(t):
                    split_rest(t)
                if attends(t):
                    mask_diagonal(t, 3)
                if prepares(t):
                    third_parts(t)

            def closing_steps():
                t = NSEQ + 1
                invert_den(NSEQ - 1)
                cut_last_inverse()
                add_attention(NSEQ)
                norm_in_statistics(t)
                divide(t, 0)
                divide(t, 1)
                norm_in(t)
                mix_tokens(t)
                add_attention(t)
                norm_in_statistics(LAST)
                choose_path(t)
                norm_in(LAST)
                mask_hidden(t, 0)
                mask_hidden(t, 1)
                mix_tokens(LAST)
                choose_path(LAST)
                mask_hidden(LAST, 2)
                mask_hidden(LAST, 3)
                add_paths(t)
                centre_out(t)
                add_paths(LAST)
                scale_out(t, 0)
                scale_out(t, 1)
                centre_out(LAST)
                scale_out(LAST, 0)
                scale_out(LAST, 1)

            norm_in_statistics(0)
            norm_in(0)
            step(0)
            for t in range(1, FIRST_LOOP):
                step(t)
            first = link.n
            with dve.Fori(FIRST_LOOP, NSEQ) as t:
                link.base, link.n = (t - FIRST_LOOP) * DVE_STEPS + first, 0
                step(t)
                assert link.n == DVE_STEPS, link.n
            link.base, link.n = first + DVE_STEPS * (NSEQ - FIRST_LOOP), 0
            step(NSEQ)
            closing_steps()

        @block.tensor
        def _(pe):
            pe.wait_ge(ident_ready, 1)

            def transpose_weights(*names):
                for name in names:
                    i = 4 * int(name[2]) if len(name) == 3 else 0
                    if name[1] == "o":
                        pe.wait_ge(wo_loaded, 16 * 2)
                        sources = [wo_in[:, c % 2, c // 2, :] for c in range(i, i + 4)]
                    else:
                        pe.wait_ge(qkv_loaded, 16 * 3)
                        sources = {"wq": [wq_in[:, c, :] for c in range(2)],
                                   "wk": [wk_in[:, c, :] for c in range(2)],
                                   "wv": [wv_in[:, c, :] for c in range(i, i + 4)]}[name[0:2]]
                    g_, done = await_bank(pe, name)
                    for c, src in enumerate(sources):
                        mm = pe.transpose(g_[:, P * c:P * (c + 1)], src, ident[:, :])
                    mm.then_inc(done, 1)

            def path_biases():
                pe.wait_ge(diag_weights_ready, 1)
                pe.wait_ge(bias_loaded, 16 * 3)
                g_, done = await_bank(pe, "bias")
                for c in range(3):
                    mm = pe.matmul(g_[0:PATHS, 0:D], b1_diag[:, c, :], w2_paths[:, c, :], start=(c == 0),
                                   stop=(c == 2))
                mm.then_inc(done, 1)

            def transpose_slab(t):
                pe.wait_ge(xn_ready, t + 1)
                g_, done = await_bank(pe, "fxt", t)
                for j in tile_range(t):
                    mm = pe.transpose(g_[:, P * j:P * (j + 1)], xn[:, j, :], ident[:, :])
                mm.then_inc(done, 1)

            xm_tiles = xm[:, :, :].rearrange("p s t -> p (s t)")

            def gate_hidden(t):
                if isinstance(t, int) and t == 0:
                    pe.wait_ge(ffn_loaded, 16 * 2)
                pe.wait_ge(xm_ready, t + 1)
                g_, done = await_bank(pe, "th", t, known=True)
                for j in tile_range(t):
                    mm = pe.matmul(g_[DM * j:DM * (j + 1), 0:P], wo1[:, :], xm_tiles[:, P * j:P * (j + 1)],
                                   start=True, stop=True, skip_group_check=True)
                mm.then_inc(done, 1)

            def gate_scores(t):
                b, n = fills_before("th", t)
                pe.wait_ge(emptied[b], n + 1)
                if isinstance(t, int) and t == 0:
                    pe.wait_ge(diag_weights_ready, 1)
                g_, done = await_bank(pe, "sc", t, known=True)
                j = tiles(t)
                rows = slice(DM * j.start, DM * j.stop)
                pe.matmul(g_[:, 0:PATHS * (j.stop - j.start)], th[rows, :],
                          wo2_diag[rows, j, :].rearrange("p j a -> p (j a)"), start=True, stop=True)\
                    .then_inc(done, 1)

            def path_hidden(t, j):
                g_, done = await_bank(pe, f"h{j}", t, known=(j == 0))
                pe.matmul(g_[:, 0:HID], xm_tiles[:, P * j:P * (j + 1)], w1[:, :, :].rearrange("p a b -> p (a b)"),
                          start=True, stop=True).then_inc(done, 1)

            def transpose_hidden(t, j):
                if not in_loop(t):
                    b, n = fills_before(f"h{j}", t)
                    pe.wait_ge(emptied[b], n + 1)
                g_, done = await_bank(pe, f"ht{j}", t)
                for c in range(3):
                    mm = pe.transpose(g_[0:KCH, P * c:P * (c + 1)], hm[:, j, KCH * c:KCH * (c + 1)], ident[:, :])
                mm.then_inc(done, 1)

            def path_out(t):
                if isinstance(t, int) and t == 0:
                    b, n = fills_before("bias", 0)
                    pe.wait_ge(emptied[b], n + 1)
                    pe.wait_ge(w2_loaded, 16 * 2)
                g_, done = await_bank(pe, "w2", t)
                for j in tile_range(t):
                    if not in_loop(t):
                        b, n = fills_before(f"ht{j}", t)
                        pe.wait_ge(emptied[b], n + 1)
                    for c in range(3):
                        mm = pe.matmul(g_[:, D * j:D * (j + 1)], hT[0:KCH, j, P * c:P * (c + 1)], w2[0:KCH, c, :],
                                       start=(c == 0), stop=(c == 2))
                mm.then_inc(done, 1)

            def scores(t, g):
                n = (t - 1) * NG + g
                if g == 0:
                    pe.wait_ge(stack_loaded, STACK_COUNT * t)
                heads = [GROUP * g + h for h in range(GROUP)]
                at = [L * (2 * (head % 8) + head // 8) for head in heads]
                pe.wait_ge(squared[1], n + 1)
                for h, a in enumerate(at):
                    mm = pe.matmul(S[:, 0, P * h:P * (h + 1)], ks[:, a + P:a + L], qs[:, a + P:a + L],
                                   start=True, stop=True)
                mm.then_inc(s_filled[0], 1)
                for h, a in enumerate(at):
                    mm = pe.matmul(S[:, 1 + h // 2, L * (h % 2):L * (h % 2 + 1)], ks[:, a:a + P], qs[:, a:a + L],
                                   start=True, stop=True)
                mm.then_inc(s_filled[1], 1)

            def values(seq, g):
                n = seq * NG + g
                if isinstance(n, int) and n == 0:
                    pe.wait_ge(const_ready, 1)
                pe.wait_ge(diag_ready, n + 1)
                pe.wait_ge(off_ready, n + 1)
                pe.wait_ge(num_ready, n + 1)
                if g == 0 and not in_loop(seq):
                    pe.wait_ge(den_ready, seq + 1)
                    for name in ("v0", "v2"):
                        b = BANK[name]
                        pe.wait_ge(emptied[b], fills_before_step(b, seq + 1))
                a = A[g % 2]
                for e in range(2):
                    for key in range(NT):
                        for j in range(GROUP):
                            col = HD * (GROUP * g + j) + HALF * e
                            pe.matmul(N[HALF * j:HALF * (j + 1), L * e + P * key:L * (e + 1)],
                                      V[:, key, col:col + HALF],
                                      a[:, 1:3, j, :] if key == 0 else a[:, 0, j, :],
                                      start=(key == 0), stop=(key == 1), skip_group_check=True)
                pe.wait_ge(sum_ready, n + 1)
                for j in range(GROUP):
                    mm = pe.matmul(Dn[HALF * j:HALF * (j + 1), 0:L], head_row[:, g, :], a[:, 1:4:2, j, :],
                                   start=(g == 0), stop=(g == NG - 1), skip_group_check=True)
                mm.then_inc(av_done, 1)

            def spread_den(t, i):
                if i == 0:
                    pe.wait_ge(rden_parts_ready, t - 1)
                g_, done = await_bank(pe, f"b{i}", t)
                for k in range(2):
                    mm = pe.matmul(g_[:, L * k:L * (k + 1)], pick_row[:, 2 * i + k, :], rden_parts[:, :], start=True,
                                   stop=True)
                mm.then_inc(done, 1)

            def project_out(t, i):
                if i == 0:
                    g_, done = await_bank(pe, "o", t)
                else:
                    b = fills_before("o", t)[0]
                    g_, done = G[b], filled[b]
                for c in range(2 * NG):
                    if i == 0 and c % NG == 0 and not (in_loop(t) and c == 0):
                        b, n = fills_before(f"b{c // NG}", t)
                        pe.wait_ge(emptied[b], n + 1)
                    mm = pe.matmul(g_[:, D * i:D * (i + 1)], yT[:, c // 2, c % 2, P * i:P * (i + 1)],
                                   woT[:, c, :], start=(c == 0), stop=(c == 2 * NG - 1))
                if i == NT - 1:
                    mm.then_inc(done, 1)

            def transpose_seq(t):
                pe.wait_ge(xa_ready, t + 1)
                g_, done = await_bank(pe, "axt", t, known=True)
                for i in range(NT):
                    mm = pe.transpose(g_[:, P * i:P * (i + 1)], xa[:, i, :], ident[:, :])
                mm.then_inc(done, 1)

            def project_qk(t):
                b, n = fills_before("axt", t)
                pe.wait_ge(emptied[b], n + 1)
                for name, w in (("q", wqT), ("k", wkT)):
                    g_, done = await_bank(pe, name, t, known=(name == "q"))
                    for c in range(2):
                        mm = pe.matmul(g_[:, L * c:L * (c + 1)], w[:, c, :, :].rearrange("p f r -> p (f r)"),
                                       xaT[:, :], start=True, stop=True)
                    mm.then_inc(done, 1)

            def project_v(t, i):
                g_, done = await_bank(pe, f"v{i}", t, known=(i == 3))
                pe.matmul(g_[:, :], xaT[:, P * (i // 2):P * (i // 2 + 1)],
                          wvT[:, 512 * (i % 2):512 * (i % 2) + 512], start=True, stop=True).then_inc(done, 1)

            def step(t):
                first = isinstance(t, int) and t == 0
                transpose_slab(t)
                if ends(t):
                    values(t - 2, 3)
                if attends(t):
                    project_v(t, 1)
                gate_hidden(t)
                if attends(t):
                    project_v(t, 3)
                gate_scores(t)
                if first:
                    path_biases()
                scores_before = tiles(t).stop - (1 if len(tile_range(t)) > NT else 2)
                for j in tile_range(t):
                    if attends(t) and j == scores_before:
                        scores(t, 0)
                    path_hidden(t, j)
                for j in tile_range(t):
                    transpose_hidden(t, j)
                if ends(t):
                    spread_den(t, 0)
                    spread_den(t, 1)
                path_out(t)
                if first:
                    transpose_weights("wq", "wk", "wv0", "wv1")
                if attends(t):
                    scores(t, 1)
                    values(t - 1, 0)
                    scores(t, 2)
                if ends(t) and not (isinstance(t, int) and t == NSEQ):
                    project_out(t, 0)
                    project_out(t, 1)
                if attends(t):
                    values(t - 1, 1)
                if prepares(t):
                    transpose_seq(t)
                if attends(t):
                    scores(t, 3)
                if prepares(t):
                    project_qk(t)
                if attends(t):
                    values(t - 1, 2)
                if prepares(t):
                    project_v(t, 0)
                    project_v(t, 2)
                if first:
                    transpose_weights("wo0", "wo1")

            def closing_steps():
                t = NSEQ + 1
                values(NSEQ - 1, 3)
                project_out(NSEQ, 0)
                project_out(NSEQ, 1)
                spread_den(t, 0)
                spread_den(t, 1)
                project_out(t, 0)
                transpose_slab(t)
                project_out(t, 1)
                gate_hidden(t)
                path_hidden(t, 0)
                gate_scores(t)
                path_hidden(t, 1)
                transpose_slab(LAST)
                transpose_hidden(t, 0)
                transpose_hidden(t, 1)
                gate_hidden(LAST)
                path_hidden(LAST, 2)
                gate_scores(LAST)
                path_hidden(LAST, 3)
                path_out(t)
                transpose_hidden(LAST, 2)
                transpose_hidden(LAST, 3)
                path_out(LAST)

            step(0)
            for t in range(1, FIRST_LOOP):
                step(t)
            with pe.Fori(FIRST_LOOP, NSEQ) as t:
                step(t)
            step(NSEQ)
            closing_steps()


_INS = ["L0_attn_hidden_states", "L0_attn_Wq", "L0_attn_Wk", "L0_attn_Wv", "L0_attn_Wo", "L0_ffn_mix_kernel",
        "L0_ffn_W1", "L0_ffn_b1", "L0_ffn_W2", "L0_ffn_b2", "L0_ffn_Wo1", "L0_ffn_bo1", "L0_ffn_Wo2",
        "L0_ffn_bo2", "L0_ffn_gamma", "L0_ffn_beta"]


def kernel(**inputs):
    import numpy as _np
    import concourse.bacc as _bacc
    from concourse import mybir as _mybir
    from concourse.bass_utils import run_bass_kernel_spmd as _run

    nc = _bacc.Bacc("TRN2", target_bir_lowering=False, num_devices=1)
    arrays, args = {}, []
    for name in _INS:
        a = _np.ascontiguousarray(inputs[name])
        arrays[f"in_{name}_dram"] = a
        args.append(nc.dram_tensor(f"in_{name}_dram", a.shape, _mybir.dt.from_np(a.dtype), kind="ExternalInput").ap())
    args.append(nc.dram_tensor("out_0_dram", (NSEQ, L, D), _mybir.dt.float32, kind="ExternalOutput").ap())
    macaron(nc, *args)
    r = _run(nc, [arrays], core_ids=[0])
    return r.results[0]["out_0_dram"]
```
